# Optimizing a Trainium2 kernel written in Bass

```python
import numpy as np
import jax
import jax.numpy as jnp

def _softmax(x, axis=-1):
    return jax.nn.softmax(x, axis=axis)

def _gelu(x):
    return jax.nn.gelu(x, approximate=True)

def _silu(x):
    return jax.nn.silu(x)

def _sigmoid(x):
    return jax.nn.sigmoid(x)

def _layernorm(x, axis=-1, eps=1e-05):
    m = jnp.mean(x, axis=axis, keepdims=True)
    v = jnp.var(x, axis=axis, keepdims=True)
    return (x - m) / jnp.sqrt(v + eps)

def _scatter_add(tgt, idx, src, axis=0):
    return tgt.at[idx].add(src)

def _segment_sum(src, seg, n):
    return jax.ops.segment_sum(src, seg, n)
kernel_name = 'mk_dlrm_tower_d1_rec_r8_28bdd8'

def setup_inputs(seed: int=0):
    np.random.seed(seed)
    _w = jnp.asarray

    def _rec_inputs():
        import jax
        import jax.numpy as jnp
        _tk = jax.random.key(seed)
        ids = jnp.stack([jax.random.randint(jax.random.fold_in(_tk, 200 + f), (512,), 0, v, jnp.int32) for f, v in enumerate([1250, 12500, 12500, 1250, 12500, 1250, 1250, 1000, 1250, 1250, 1000, 1250, 1250, 1000, 1000, 125000, 125000, 1000, 12500, 1250, 1250, 1000, 125000, 12500, 12500, 1000])], axis=1)
        tbl_0 = 0.05 * jax.random.normal(jax.random.fold_in(_tk, 500 + 0), (1250, 64), jnp.float32)
        tbl_1 = 0.05 * jax.random.normal(jax.random.fold_in(_tk, 500 + 1), (12500, 64), jnp.float32)
        tbl_2 = 0.05 * jax.random.normal(jax.random.fold_in(_tk, 500 + 2), (12500, 64), jnp.float32)
        tbl_3 = 0.05 * jax.random.normal(jax.random.fold_in(_tk, 500 + 3), (1250, 64), jnp.float32)
        tbl_4 = 0.05 * jax.random.normal(jax.random.fold_in(_tk, 500 + 4), (12500, 64), jnp.float32)
        tbl_5 = 0.05 * jax.random.normal(jax.random.fold_in(_tk, 500 + 5), (1250, 64), jnp.float32)
        tbl_6 = 0.05 * jax.random.normal(jax.random.fold_in(_tk, 500 + 6), (1250, 64), jnp.float32)
        tbl_7 = 0.05 * jax.random.normal(jax.random.fold_in(_tk, 500 + 7), (1000, 64), jnp.float32)
        tbl_8 = 0.05 * jax.random.normal(jax.random.fold_in(_tk, 500 + 8), (1250, 64), jnp.float32)
        tbl_9 = 0.05 * jax.random.normal(jax.random.fold_in(_tk, 500 + 9), (1250, 64), jnp.float32)
        tbl_10 = 0.05 * jax.random.normal(jax.random.fold_in(_tk, 500 + 10), (1000, 64), jnp.float32)
        tbl_11 = 0.05 * jax.random.normal(jax.random.fold_in(_tk, 500 + 11), (1250, 64), jnp.float32)
        tbl_12 = 0.05 * jax.random.normal(jax.random.fold_in(_tk, 500 + 12), (1250, 64), jnp.float32)
        tbl_13 = 0.05 * jax.random.normal(jax.random.fold_in(_tk, 500 + 13), (1000, 64), jnp.float32)
        tbl_14 = 0.05 * jax.random.normal(jax.random.fold_in(_tk, 500 + 14), (1000, 64), jnp.float32)
        tbl_15 = 0.05 * jax.random.normal(jax.random.fold_in(_tk, 500 + 15), (125000, 64), jnp.float32)
        tbl_16 = 0.05 * jax.random.normal(jax.random.fold_in(_tk, 500 + 16), (125000, 64), jnp.float32)
        tbl_17 = 0.05 * jax.random.normal(jax.random.fold_in(_tk, 500 + 17), (1000, 64), jnp.float32)
        tbl_18 = 0.05 * jax.random.normal(jax.random.fold_in(_tk, 500 + 18), (12500, 64), jnp.float32)
        tbl_19 = 0.05 * jax.random.normal(jax.random.fold_in(_tk, 500 + 19), (1250, 64), jnp.float32)
        tbl_20 = 0.05 * jax.random.normal(jax.random.fold_in(_tk, 500 + 20), (1250, 64), jnp.float32)
        tbl_21 = 0.05 * jax.random.normal(jax.random.fold_in(_tk, 500 + 21), (1000, 64), jnp.float32)
        tbl_22 = 0.05 * jax.random.normal(jax.random.fold_in(_tk, 500 + 22), (125000, 64), jnp.float32)
        tbl_23 = 0.05 * jax.random.normal(jax.random.fold_in(_tk, 500 + 23), (12500, 64), jnp.float32)
        tbl_24 = 0.05 * jax.random.normal(jax.random.fold_in(_tk, 500 + 24), (12500, 64), jnp.float32)
        tbl_25 = 0.05 * jax.random.normal(jax.random.fold_in(_tk, 500 + 25), (1000, 64), jnp.float32)
        _rk = jax.random.fold_in(_tk, 7)
        r_dense_t = 7.22013e-05 + 1.00017 * jax.random.normal(jax.random.fold_in(_rk, 101), (512, 256), jnp.float32)
        W_top1 = 0.0360844 * jax.random.normal(jax.random.fold_in(_tk, 801), (768, 512), jnp.float32)
        W_top2 = 0.0441942 * jax.random.normal(jax.random.fold_in(_tk, 802), (512, 256), jnp.float32)
        W_top3 = 0.0625 * jax.random.normal(jax.random.fold_in(_tk, 803), (256, 1), jnp.float32)
        b_top1 = jnp.zeros((512,), jnp.float32)
        b_top2 = jnp.zeros((256,), jnp.float32)
        return (r_dense_t, ids, tbl_0, tbl_1, tbl_2, tbl_3, tbl_4, tbl_5, tbl_6, tbl_7, tbl_8, tbl_9, tbl_10, tbl_11, tbl_12, tbl_13, tbl_14, tbl_15, tbl_16, tbl_17, tbl_18, tbl_19, tbl_20, tbl_21, tbl_22, tbl_23, tbl_24, tbl_25, W_top1, b_top1, W_top2, b_top2, W_top3)
    r_dense_t, ids, tbl_0, tbl_1, tbl_2, tbl_3, tbl_4, tbl_5, tbl_6, tbl_7, tbl_8, tbl_9, tbl_10, tbl_11, tbl_12, tbl_13, tbl_14, tbl_15, tbl_16, tbl_17, tbl_18, tbl_19, tbl_20, tbl_21, tbl_22, tbl_23, tbl_24, tbl_25, W_top1, b_top1, W_top2, b_top2, W_top3 = _rec_inputs()

    def _L0_rec_setup():
        import jax, jax.numpy as jnp
        import numpy as np
        EPS = 1e-05
        NI = 33
        TRIL_I, TRIL_J = np.tril_indices(NI, k=-1)

        def layer_norm(x, g, b):
            m = jnp.mean(x, axis=-1, keepdims=True)
            v = jnp.mean(jnp.square(x - m), axis=-1, keepdims=True)
            return (x - m) * jax.lax.rsqrt(v + EPS) * g + b
        key = jax.random.key(seed)
        ks = jax.random.split(key, 8)
        B, D_DENSE, N_SP, D_SP = (4096, 256, 26, 64)
        E, PROJ, MAXD, NFLAT = (128, 32, 512, 528)
        dense_t = jax.random.normal(ks[0], (B, D_DENSE), dtype=jnp.float32)
        sparse_t = jax.random.normal(ks[1], (B, N_SP, D_SP), dtype=jnp.float32)
        Wd = jax.random.normal(ks[2], (E, D_DENSE), dtype=jnp.float32) / np.sqrt(D_DENSE)
        Ws = jax.random.normal(ks[3], (E, D_SP), dtype=jnp.float32) / np.sqrt(D_SP)
        Wsi = jax.random.normal(ks[4], (PROJ, N_SP), dtype=jnp.float32) / np.sqrt(N_SP)
        Wl = jax.random.normal(ks[5], (MAXD, NFLAT), dtype=jnp.float32) / np.sqrt(NFLAT)
        gd = jnp.ones((E,), jnp.float32)
        bd = jnp.zeros((E,), jnp.float32)
        gs = jnp.ones((E,), jnp.float32)
        bs = jnp.zeros((E,), jnp.float32)
        gsi = jnp.ones((PROJ,), jnp.float32)
        bsi = jnp.zeros((PROJ,), jnp.float32)
        gl = jnp.ones((MAXD,), jnp.float32)
        bl = jnp.zeros((MAXD,), jnp.float32)
        return {'dense_t': dense_t, 'sparse_t': sparse_t, 'Wd': Wd, 'gd': gd, 'bd': bd, 'Ws': Ws, 'gs': gs, 'bs': bs, 'Wsi': Wsi, 'gsi': gsi, 'bsi': bsi, 'Wl': Wl, 'gl': gl, 'bl': bl, 'dims_in_use': 384}
    _L0_rec_all = _L0_rec_setup()
    _L0_rec_in = {k: v for k, v in _L0_rec_all.items() if k in ('Wd', 'gd', 'bd', 'Ws', 'gs', 'bs', 'Wsi', 'gsi', 'bsi', 'Wl', 'gl', 'bl')}
    del _L0_rec_all
    return {'r_dense_t': r_dense_t, 'ids': ids, 'tbl_0': tbl_0, 'tbl_1': tbl_1, 'tbl_2': tbl_2, 'tbl_3': tbl_3, 'tbl_4': tbl_4, 'tbl_5': tbl_5, 'tbl_6': tbl_6, 'tbl_7': tbl_7, 'tbl_8': tbl_8, 'tbl_9': tbl_9, 'tbl_10': tbl_10, 'tbl_11': tbl_11, 'tbl_12': tbl_12, 'tbl_13': tbl_13, 'tbl_14': tbl_14, 'tbl_15': tbl_15, 'tbl_16': tbl_16, 'tbl_17': tbl_17, 'tbl_18': tbl_18, 'tbl_19': tbl_19, 'tbl_20': tbl_20, 'tbl_21': tbl_21, 'tbl_22': tbl_22, 'tbl_23': tbl_23, 'tbl_24': tbl_24, 'tbl_25': tbl_25, 'W_top1': W_top1, 'b_top1': b_top1, 'W_top2': W_top2, 'b_top2': b_top2, 'W_top3': W_top3, 'L0_rec_Wd': _L0_rec_in['Wd'], 'L0_rec_gd': _L0_rec_in['gd'], 'L0_rec_bd': _L0_rec_in['bd'], 'L0_rec_Ws': _L0_rec_in['Ws'], 'L0_rec_gs': _L0_rec_in['gs'], 'L0_rec_bs': _L0_rec_in['bs'], 'L0_rec_Wsi': _L0_rec_in['Wsi'], 'L0_rec_gsi': _L0_rec_in['gsi'], 'L0_rec_bsi': _L0_rec_in['bsi'], 'L0_rec_Wl': _L0_rec_in['Wl'], 'L0_rec_gl': _L0_rec_in['gl'], 'L0_rec_bl': _L0_rec_in['bl']}

def reference(r_dense_t, ids, tbl_0, tbl_1, tbl_2, tbl_3, tbl_4, tbl_5, tbl_6, tbl_7, tbl_8, tbl_9, tbl_10, tbl_11, tbl_12, tbl_13, tbl_14, tbl_15, tbl_16, tbl_17, tbl_18, tbl_19, tbl_20, tbl_21, tbl_22, tbl_23, tbl_24, tbl_25, W_top1, b_top1, W_top2, b_top2, W_top3, L0_rec_Wd, L0_rec_gd, L0_rec_bd, L0_rec_Ws, L0_rec_gs, L0_rec_bs, L0_rec_Wsi, L0_rec_gsi, L0_rec_bsi, L0_rec_Wl, L0_rec_gl, L0_rec_bl):
    import jax
    import jax.numpy as jnp

    def _L0_rec_ref(dense_t, sparse_t, Wd, gd, bd, Ws, gs, bs, Wsi, gsi, bsi, Wl, gl, bl, dims_in_use):
        import jax, jax.numpy as jnp
        import numpy as np
        EPS = 1e-05
        NI = 33
        TRIL_I, TRIL_J = np.tril_indices(NI, k=-1)

        def layer_norm(x, g, b):
            m = jnp.mean(x, axis=-1, keepdims=True)
            v = jnp.mean(jnp.square(x - m), axis=-1, keepdims=True)
            return (x - m) * jax.lax.rsqrt(v + EPS) * g + b
        x = layer_norm(dense_t @ Wd.T, gd, bd)
        y = layer_norm(jnp.einsum('bnd,ed->bne', sparse_t, Ws), gs, bs)
        y = jnp.einsum('bne,pn->bep', y, Wsi)
        y = layer_norm(y, gsi, bsi)
        y = jnp.swapaxes(y, 1, 2)
        T = jnp.concatenate([x[:, None, :], y], axis=1)
        Z = jnp.einsum('bnd,bmd->bnm', T, T)
        Zflat = Z[:, TRIL_I, TRIL_J]
        out = layer_norm(Zflat @ Wl.T, gl, bl)
        maxd = out.shape[-1]
        mask = (jnp.arange(maxd) < dims_in_use).astype(out.dtype)
        return out * mask
    e = jnp.stack([tbl_0[ids[:, 0]], tbl_1[ids[:, 1]], tbl_2[ids[:, 2]], tbl_3[ids[:, 3]], tbl_4[ids[:, 4]], tbl_5[ids[:, 5]], tbl_6[ids[:, 6]], tbl_7[ids[:, 7]], tbl_8[ids[:, 8]], tbl_9[ids[:, 9]], tbl_10[ids[:, 10]], tbl_11[ids[:, 11]], tbl_12[ids[:, 12]], tbl_13[ids[:, 13]], tbl_14[ids[:, 14]], tbl_15[ids[:, 15]], tbl_16[ids[:, 16]], tbl_17[ids[:, 17]], tbl_18[ids[:, 18]], tbl_19[ids[:, 19]], tbl_20[ids[:, 20]], tbl_21[ids[:, 21]], tbl_22[ids[:, 22]], tbl_23[ids[:, 23]], tbl_24[ids[:, 24]], tbl_25[ids[:, 25]]], axis=1)
    z = _L0_rec_ref(r_dense_t, e, L0_rec_Wd, L0_rec_gd, L0_rec_bd, L0_rec_Ws, L0_rec_gs, L0_rec_bs, L0_rec_Wsi, L0_rec_gsi, L0_rec_bsi, L0_rec_Wl, L0_rec_gl, L0_rec_bl, 384)
    z = z.reshape(z.shape[0], -1)
    h = jnp.concatenate([z, r_dense_t], axis=1)
    h = jnp.maximum(h @ W_top1 + b_top1, 0.0)
    h = jnp.maximum(h @ W_top2 + b_top2, 0.0)
    y = h @ W_top3
    return y

_drawn_inputs = setup_inputs


def setup_inputs(seed=0):
    import zlib

    import numpy as np

    out = dict(_drawn_inputs(seed))
    spreads = {'b_top1': (0.0, 0.1),
     'b_top2': (0.0, 0.1),
     'L0_rec_gd': (1.0, 0.6),
     'L0_rec_bd': (0.0, 0.8),
     'L0_rec_gs': (1.0, 0.6),
     'L0_rec_bs': (0.0, 0.1),
     'L0_rec_gsi': (1.0, 0.2),
     'L0_rec_bsi': (0.0, 0.1),
     'L0_rec_gl': (1.0, 0.2),
     'L0_rec_bl': (0.0, 0.1)}
    factors = {}
    for name, (base, spread) in spreads.items():
        noise = np.random.default_rng([zlib.crc32(name.encode()), seed]).standard_normal(out[name].shape)
        drawn = base * np.exp(spread * noise) if base else spread * noise
        out[name] = jnp.asarray(drawn.astype(out[name].dtype))
    for name, factor in factors.items():
        out[name] = (out[name] * factor).astype(out[name].dtype)
    return out
```

```python
from contextlib import ExitStack

import numpy as np
import concourse.bass as bass
from concourse import mybir

ALU = mybir.AluOpType
ACT = mybir.ActivationFunctionType
AX_X = mybir.AxisListType.X
F32 = mybir.dt.float32
BF16 = mybir.dt.bfloat16
I32 = mybir.dt.int32

P = 128
EPS = 1e-5
B = 512
NF = 26
D = 64
E = 128
PR = 32
DENSE = 256
OUT = 512
KEPT = 384
H1 = 512
H2 = 256

GROUP = 128
NG = B // GROUP
TILES = GROUP * NF // P
PAIRS = TILES // 2
HALF = TILES // 2
QS = 16
QUARTERS = GROUP // QS
ITEMS = PR + 2
SLOTS = QS // 2
NZ = GROUP // 2
LOW = PR // 2
KL = LOW // 4
KC = KL + LOW // 8
ROW_ONE, ROW_S, ROW_XS = 32, 64, 96
ROWS_X = ROW_XS + 1


def span(tile):
    k = tile % HALF
    return P * k // NF, (P * k + P - 1) // NF


SPANS = [span(k)[1] - span(k)[0] + 1 for k in range(HALF)]
AT = [sum(SPANS[:k]) for k in range(HALF)]
NSPAN = sum(SPANS)


def pieces(tile):
    lo, hi = span(tile)
    base = (tile // HALF) * (HALF * P // NF)
    out = []
    for q in range(QUARTERS):
        a, b = max(base + lo, QS * q), min(base + hi, QS * q + QS - 1)
        if a <= b:
            out.append((q, (a - QS * q) * PR, (b - a + 1) * PR, (AT[tile % HALF] + a - base - lo) * PR))
    return out


LAST_PAIR = [((QS * NF * (q + 1) - 1) // P) // 2 for q in range(QUARTERS)]
FIRST_TILE = [QS * NF * q // P for q in range(QUARTERS)]
LAG = 2


def gram_entry(p, k):
    if k < KL:
        return p % PR, 4 * k + p // PR
    return LOW + p % LOW, LOW + 8 * (k - KL) + p // LOW


def bank(j):
    return j % 3 if j < PAIRS - 1 else 1


def bank_before(j):
    return {0: 4, 1: 2, PAIRS - 1: 2}.get(j, 3)


def dlrm_tower(nc, t):
    ctx = ExitStack()
    with ctx:
        def sb(name, shape, dt=F32):
            return ctx.enter_context(nc.sbuf_tensor(name, shape, dt))

        def pb(name, shape):
            return ctx.enter_context(nc.psum_tensor(name, shape, F32))

        def sem(name):
            return ctx.enter_context(nc.semaphore(name))

        ids = sb("ids_sb", [P, NG * TILES], I32)
        bases = sb("bases_sb", [P, HALF], I32)
        rows_at = sb("rows_at", [P, 2, HALF], I32)
        emb = sb("emb", [P, TILES, D])
        embT = sb("embT", [P, PAIRS, P])
        proj = sb("proj", [P, PAIRS, 2, E])
        junk = sb("junk", [P, 2, E])
        u_ms = sb("u_ms", [P, PAIRS, 2])
        u_sd = sb("u_sd", [P, PAIRS, 2])
        u_r = sb("u_r", [P, PAIRS, 2])
        ysq = sb("ysq", [P, 2, QS, PR])
        y_ms = sb("y_ms", [P, QUARTERS, QS])
        y_sd = sb("y_sd", [P, QUARTERS, QS])
        y_r = sb("y_r", [P, QUARTERS, QS])
        T = sb("T", [P, GROUP, ITEMS])
        gram = sb("gram", [2 * PR, ITEMS, NZ])
        zn = sb("zn", [P, KC, 2, NZ])
        zx = sb("zx", [P, 2, NZ])
        f_bn = sb("f_bn", [P, 6])
        f_mv = sb("f_mv", [P, 2])
        f_sd = sb("f_sd", [P, 1])
        f_r = sb("f_r", [P, 1])
        znorm = sb("znorm", [P, KEPT])
        zT = sb("zT", [P, KEPT // P, GROUP])
        h1 = sb("h1", [P, H1 // P, GROUP])
        h2 = sb("h2", [P, H2 // P, GROUP])
        y_row = sb("y_row", [1, B])
        wbd = sb("wbd", [P, NSPAN, PR])
        wbd_m = sb("wbd_m", [P, NSPAN])
        wsT = sb("wsT", [P, 2, E])
        ws_m = sb("ws_m", [P, 2])
        gs_b = sb("gs_b", [P, E])
        wsiT = sb("wsiT", [NF, PR])
        wsi_m = sb("wsi_m", [NF, 1])
        bs9 = sb("bs9", [9, E])
        sel9 = sb("sel9", [9, 6])
        sc9 = sb("sc9", [9, PR])
        part = sb("part", [9, 3, E], BF16)
        rest = sb("rest", [9, 2, E])
        acc9 = sb("acc9", [9, E])
        bias_l = sb("bias_l", [9, E], BF16)
        bias_r = sb("bias_r", [9, QS, PR], BF16)
        wdT = sb("wdT", [P, DENSE // P, E])
        wd_m = sb("wd_m", [P, DENSE // P])
        denseT = sb("denseT", [P, DENSE // P, B])
        gdbd = sb("gdbd", [P, 2])
        xsq = sb("xsq", [P, B])
        x_r = sb("x_r", [P, B])
        xT = sb("xT", [P, B])
        xs = sb("xs", [P, NG, 2, NZ])
        wl = sb("wl", [P, KC, OUT])
        wlx = sb("wlx", [PR, OUT])
        wl5 = sb("wl5", [P, OUT])
        gb = sb("gb", [P, 4, KC])
        gg = sb("gg", [P, 4, KC])
        sel = sb("sel", [P, 2, KC, PR])
        fold = sb("fold", [P, KC, ROWS_X])
        foldx = sb("foldx", [PR, ROWS_X])
        gbsi = sb("gbsi", [PR, 2])
        glbl = sb("glbl", [P, 2, KEPT // P])
        w1 = sb("w1", [P, (KEPT + DENSE) // P, H1])
        b1 = sb("b1", [P, H1 // P])
        w2 = sb("w2", [P, H1 // P, H2])
        b2 = sb("b2", [P, H2 // P])
        w3 = sb("w3", [P, H2 // P])
        ident = sb("ident", [P, P])
        ones = sb("ones", [P, 9])
        mean_w = sb("mean_w", [P, P])
        eps = sb("eps", [P, 1])

        TU = [pb(f"tu{i}", [P, 512]) for i in range(3)]
        PY = [pb(f"py{i}", [P, QS, PR]) for i in range(2)]
        PZ = pb("pz", [P, 512])
        PZv = PZ[:, 0:SLOTS * ITEMS].rearrange("p (b c) -> p b c", c=ITEMS)
        PF = pb("pf", [P, 512])
        PM = pb("pm", [P, 512])

        l_ids = sem("l_ids")
        l_proj = sem("l_proj")
        l_comb = sem("l_comb")
        l_dense = sem("l_dense")
        l_late = sem("l_late")
        rows_ready = sem("rows_ready")
        rows_seen = sem("rows_seen")
        gathered = [sem(f"gathered{j}") for j in range(PAIRS)]
        consts_ready = sem("consts_ready")
        t_done = sem("t_done")
        u_done = sem("u_done")
        y_done = sem("y_done")
        z_done = sem("z_done")
        f_done = sem("f_done")
        tz_done = sem("tz_done")
        m1_done = sem("m1_done")
        m2_done = sem("m2_done")
        m3_done = sem("m3_done")
        x_done = sem("x_done")
        sc_done = sem("sc_done")
        xs_done = sem("xs_done")
        w5_done = sem("w5_done")
        embT_ready = sem("embT_ready")
        u_ms_ready = sem("u_ms_ready")
        u_sd_ready = sem("u_sd_ready")
        ysq_ready = sem("ysq_ready")
        y_sd_ready = sem("y_sd_ready")
        xcol_ready = sem("xcol_ready")
        gram_ready = sem("gram_ready")
        f_sd_ready = sem("f_sd_ready")
        zT_ready = sem("zT_ready")
        h1_ready = sem("h1_ready")
        h2_ready = sem("h2_ready")
        y_ready = sem("y_ready")
        xsq_ready = sem("xsq_ready")
        x_sd_ready = sem("x_sd_ready")
        xs_ready = sem("xs_ready")
        zx_xs_ready = sem("zx_xs_ready")
        wl5_ready = sem("wl5_ready")
        dve_setup = sem("dve_setup")
        wsT_ready = sem("wsT_ready")
        wbd_ready = sem("wbd_ready")
        wsi_ready = sem("wsi_ready")
        wd_ready = sem("wd_ready")
        bias_ready = sem("bias_ready")
        xT_ready = sem("xT_ready")
        wl_ready = sem("wl_ready")
        fold_ready = sem("fold_ready")
        u_r_ready = sem("u_r_ready")
        proj_ready = sem("proj_ready")
        y_ms_ready = sem("y_ms_ready")
        y_r_ready = sem("y_r_ready")
        T_ready = sem("T_ready")
        f_bn_ready = sem("f_bn_ready")
        f_bn_seen = sem("f_bn_seen")
        f_mv_ready = sem("f_mv_ready")
        f_r_ready = sem("f_r_ready")
        znorm_ready = sem("znorm_ready")
        stacked = [sem(f"stacked{i}") for i in range(2)]
        stored = sem("stored")

        HALF_DMAS = 16 * 2 * (4 + 8 + 2)

        block = ctx.enter_context(nc.Block())

        @block.sync
        def _(sp):
            sp.dma_start(ids[:, :], t["ids"]).then_inc(l_ids, 16)
            sp.dma_start(bases[:, :], t["bases"]).then_inc(l_ids, 16)
            sp.dma_start(ident[:, :], t["ident"]).then_inc(l_proj, 16)
            sp.dma_start(wsT[:, :, :], t["wsT"]).then_inc(l_proj, 16)
            sp.dma_start(gs_b[:, :], t["gs"].partition_broadcast(P)).then_inc(l_proj, 16)
            sp.dma_start(wdT[:, :, :], t["wdT"]).then_inc(l_dense, 16)
            sp.dma_start(denseT[:, :, :], t["denseT"]).then_inc(l_dense, 16)
            sp.dma_start(gdbd[:, :], t["gdbd"]).then_inc(l_dense, 16)
            for dst, src in ((wl, "wl"), (wlx, "wlx"), (gb, "gb"), (sel, "sel"), (gbsi, "gbsi"),
                             (glbl, "glbl"), (w1, "w1"), (b1, "b1"), (w2, "w2"), (b2, "b2"), (w3, "w3")):
                sp.dma_start(dst[tuple(slice(None) for _ in dst.shape)], t[src]).then_inc(l_late, 16)

            def stack_half(g, hf):
                sp.wait_ge(gram_ready, QUARTERS * g + (QUARTERS // 2) * (hf + 1))
                at = slice(NZ // 2 * hf, NZ // 2 * (hf + 1))
                for h in range(2):
                    lo = gram[PR * h:PR * h + PR, :, at]
                    hi = gram[PR * h + LOW:PR * h + PR, :, at]
                    for r in range(4):
                        sp.dma_start(zn[PR * r:PR * r + PR, 0:KL, h, at], lo[:, r:LOW:4, :]).then_inc(stacked[hf], 16)
                    for r in range(8):
                        sp.dma_start(zn[LOW * r:LOW * r + LOW, KL:KC, h, at],
                                     hi[:, LOW + r:PR:8, :]).then_inc(stacked[hf], 16)
                    sp.dma_start(zx[0:PR, h, at], lo[:, PR, :]).then_inc(stacked[hf], 16)
                    sp.dma_start(zx[ROW_S:ROW_S + PR, h, at], lo[:, PR + 1, :]).then_inc(stacked[hf], 16)

            sp.wait_ge(consts_ready, 6)
            stack_half(0, 0)
            stack_half(0, 1)
            with sp.Fori(1, NG) as g:
                sp.wait_ge(f_done, g)
                stack_half(g, 0)
                stack_half(g, 1)
            sp.wait_ge(y_ready, NG)
            sp.dma_start(t["out"].rearrange("b one -> one b"), y_row[:, :]).then_inc(stored, 16)
            sp.wait_ge(stored, 16)

        @block.gpsimd
        def _(pool):
            pool.memset(eps[:, :], EPS).then_inc(consts_ready, 1)
            pool.memset(mean_w[:, :], 1.0 / E).then_inc(consts_ready, 1)
            pool.memset(ones[:, :], 1.0).then_inc(consts_ready, 1)
            pool.wait_ge(l_ids, 32)

            def gather_half(g, half, later):
                if later:
                    pool.wait_ge(t_done, (g - 1) * PAIRS + (HALF + 1) // 2 + half * (HALF // 2))
                pool.tensor_tensor(rows_at[:, half, :], ids[:, bass.ds(g * TILES + half * HALF, HALF)],
                                   bases[:, :], ALU.add).then_inc(rows_ready, 1)
                pool.wait_ge(rows_ready, g * 2 + half + 1)
                pool.sem_inc(rows_seen, 1)
                for k in range(half * HALF, (half + 1) * HALF):
                    pool.indirect_dma_start(
                        emb[:, k, :], None, t["tables"],
                        bass.IndirectOffsetOnAxis(ap=rows_at[:, half, k - half * HALF:k - half * HALF + 1], axis=0),
                    ).then_inc(gathered[k // 2], 16)

            gather_half(0, 0, False)
            pool.memset(zx[:, :, :], 0.0).then_inc(consts_ready, 1)
            pool.wait_ge(consts_ready, 4)
            pool.memset(T[:, :, PR + 1:PR + 2], 1.0).then_inc(consts_ready, 1)
            pool.wait_ge(consts_ready, 5)
            pool.memset(zx[ROW_ONE:ROW_ONE + 1, :, :], 1.0).then_inc(consts_ready, 1)
            pool.wait_ge(consts_ready, 6)
            gather_half(0, 1, False)
            with pool.Fori(1, NG) as g:
                gather_half(g, 0, True)
                gather_half(g, 1, True)

        @block.tensor
        def _(pe):
            def transposes(g, j, later):
                pe.wait_ge(gathered[j], g * 32 + 32)
                if later or j >= 3:
                    pe.wait_ge(proj_ready, g * PAIRS + j + 1 - bank_before(j))
                pe.transpose(TU[bank(j)][:, 0:P], emb[:, 2 * j:2 * j + 2, :].rearrange("p t d -> p (t d)"),
                             ident[:, :]).then_inc(t_done, 1)

            def project(g, j):
                pe.wait_ge(embT_ready, g * PAIRS + j + 1)
                pe.matmul(TU[bank(j)][:, P:P + 2 * E], embT[:, j, :], wsT[:, :, :].rearrange("p t e -> p (t e)"),
                          start=True, stop=True).then_inc(u_done, 1)

            def combine(g, j, later):
                pe.wait_ge(proj_ready, g * PAIRS + j + 1)
                for tile in (2 * j, 2 * j + 1):
                    for q, col, n, at in pieces(tile):
                        if tile == FIRST_TILE[q]:
                            if later or q >= 2:
                                pe.wait_ge(T_ready, g * QUARTERS + q - 1)
                            pe.matmul(PY[q % 2][:, :, :].rearrange("p b c -> p (b c)"), bias_l[:, :],
                                      bias_r[:, :, :].rearrange("p b c -> p (b c)"),
                                      start=True, stop=False, skip_group_check=True)
                        mm = pe.matmul(PY[q % 2][:, :, :].rearrange("p b c -> p (b c)")[:, col:col + n],
                                       proj[:, j, tile % 2, :],
                                       wbd[:, :, :].rearrange("p b c -> p (b c)")[:, at:at + n],
                                       start=False, stop=col + n == QS * PR, skip_group_check=True)
                mm.then_inc(y_done, 1)

            def gram_products(g, q, later):
                pe.wait_ge(T_ready, g * QUARTERS + q + 1)
                if q == 0:
                    pe.wait_ge(xcol_ready, g + 1)
                if later or q >= 1:
                    pe.wait_ge(gram_ready, g * QUARTERS + q)
                for s in range(QS):
                    h, b = s % 2, s // 2
                    of = T[:, QS * q + s, 0:ITEMS]
                    mm = pe.matmul(PZ[PR * h:PR * h + PR, ITEMS * b:ITEMS * (b + 1)], of[:, 0:PR], of,
                                   start=True, stop=True)
                mm.then_inc(z_done, 1)

            def flat_layer(g, later):
                pe.wait_ge(stacked[0], g * HALF_DMAS + HALF_DMAS)
                pe.wait_ge(stacked[1], g * HALF_DMAS + HALF_DMAS)
                pe.wait_ge(zx_xs_ready, g + 1)
                if later:
                    pe.wait_ge(y_ready, g)
                for k in range(KC):
                    pe.matmul(PF[:, :], zn[:, k, :, :].rearrange("p h b -> p (h b)"), wl[:, k, :],
                              start=(k == 0), stop=False)
                pe.matmul(PF[:, :], zx[0:ROWS_X, :, :].rearrange("p h b -> p (h b)"), wl5[0:ROWS_X, :],
                          start=False, stop=True).then_inc(f_done, 1)

            def z_transposes(g):
                pe.wait_ge(znorm_ready, g + 1)
                for c in range(KEPT // P):
                    mm = pe.transpose(PM[:, P * c:P * c + P], znorm[:, P * c:P * c + P], ident[:, :])
                mm.then_inc(tz_done, 1)

            def mlp1(g):
                pe.wait_ge(zT_ready, g + 1)
                for m in range(H1 // P):
                    for n, c in enumerate((3, 4, 0, 1, 2)):
                        rhs = zT[:, c, :] if c < 3 else denseT[:, c - 3, bass.ds(g * GROUP, GROUP)]
                        mm = pe.matmul(PF[:, P * m:P * m + P], w1[:, c, P * m:P * m + P], rhs,
                                       start=(n == 0), stop=(n == 4))
                mm.then_inc(m1_done, 1)

            def mlp2(g):
                pe.wait_ge(h1_ready, g + 1)
                for m in range(H2 // P):
                    for c in range(H1 // P):
                        mm = pe.matmul(PM[:, P * m:P * m + P], w2[:, c, P * m:P * m + P], h1[:, c, :],
                                       start=(c == 0), stop=(c == H1 // P - 1))
                mm.then_inc(m2_done, 1)

            def mlp3(g):
                pe.wait_ge(h2_ready, g + 1)
                for c in range(H2 // P):
                    mm = pe.matmul(PF[0:1, 0:GROUP], w3[:, c:c + 1], h2[:, c, :],
                                   start=(c == 0), stop=(c == H2 // P - 1))
                mm.then_inc(m3_done, 1)

            def before(g, step, later):
                if step in (0, 1):
                    gram_products(g, QUARTERS - 2 + step, True)
                if step == 5:
                    flat_layer(g, later)
                if step == 7:
                    z_transposes(g)
                if step == 8:
                    mlp1(g)
                if step == 10:
                    mlp2(g)
                if step == 11:
                    mlp3(g)

            def x_side():
                pe.wait_ge(wd_ready, 1)
                for c in range(DENSE // P):
                    mm = pe.matmul(PF[:, :], wdT[:, c, :], denseT[:, c, :], start=(c == 0), stop=(c == 1))
                mm.then_inc(x_done, 1)
                pe.wait_ge(wsi_ready, 1)
                pe.matmul(PZ[0:9, 0:PR], ones[0:NF, :], wsiT[:, :], start=True, stop=True).then_inc(sc_done, 1)
                pe.wait_ge(xsq_ready, 1)
                pe.matmul(PM[:, :], mean_w[:, :], xsq[:, :], start=True, stop=True).then_inc(x_done, 1)

            def folded_weights():
                pe.wait_ge(xT_ready, 1)
                pe.matmul(PM[0:1, :], ones[:, 0:1], xT[:, :], start=True, stop=True).then_inc(xs_done, 1)
                pe.wait_ge(fold_ready, 1)
                for k in range(KC):
                    pe.matmul(PF[0:ROWS_X, :], fold[:, k, :], wl[:, k, :], start=(k == 0), stop=False)
                pe.matmul(PF[0:ROWS_X, :], foldx[:, :], wlx[:, :], start=False, stop=True).then_inc(w5_done, 1)

            def group(g, later):
                transposes(g, 0, later)
                transposes(g, 1, later)
                project(g, 0)
                for j in range(PAIRS):
                    if j + 2 < PAIRS:
                        transposes(g, j + 2, later)
                    if j + 1 < PAIRS:
                        project(g, j + 1)
                    combine(g, j, later)
                    if later:
                        before(g - 1, j, True if j < 5 else True)
                    elif j == 8:
                        folded_weights()
                    for q in range(QUARTERS):
                        if LAST_PAIR[q] + LAG == j:
                            gram_products(g, q, later)

            pe.wait_ge(consts_ready, 3)
            pe.wait_ge(l_proj, 48)
            pe.wait_ge(wsT_ready, 1)
            x_side()
            pe.wait_ge(bias_ready, 1)
            pe.wait_ge(wbd_ready, 1)
            group(0, False)
            pe.wait_ge(wl5_ready, 1)
            pe.wait_ge(wl_ready, 1)
            with pe.Fori(1, NG) as g:
                group(g, True)
            for step in range(PAIRS):
                before(NG - 1, step, True)

        @block.scalar
        def _(act):
            act.dma_start(wbd[:, :, :], t["wbd"]).then_inc(l_comb, 16)
            act.dma_start(wsiT[:, :], t["wsiT"]).then_inc(l_comb, 16)
            act.dma_start(bs9[:, :], t["bs"].partition_broadcast(9)).then_inc(l_comb, 16)
            act.dma_start(sel9[:, :], t["sel9"]).then_inc(l_comb, 16)

            def embT_copy(g, j):
                act.wait_ge(t_done, g * PAIRS + j + 1)
                act.activation(embT[:, j, :], TU[bank(j)][:, 0:P], ACT.Copy).then_inc(embT_ready, 1)

            def u_spread(g, j):
                act.wait_ge(u_done, g * PAIRS + j + 1)
                for i in range(2):
                    a = act.activation(junk[:, i, :], TU[bank(j)][:, P + E * i:P + E * (i + 1)], ACT.Square,
                                       scale=float(E) ** -0.5, accum_out=u_ms[:, j, i:i + 1])
                a.then_inc(u_ms_ready, 1)
                act.wait_ge(u_ms_ready, g * PAIRS + j + 1)
                act.activation(u_sd[:, j, :], u_ms[:, j, :], ACT.Sqrt, bias=eps[:, :]).then_inc(u_sd_ready, 1)

            def y_square(g, q):
                act.wait_ge(y_done, g * PAIRS + LAST_PAIR[q] + 1)
                act.activation(ysq[:, q % 2, :, :], PY[q % 2][:, :, :], ACT.Square,
                               scale=float(PR) ** -0.5).then_inc(ysq_ready, 1)

            def y_spread(g, q):
                act.wait_ge(y_ms_ready, g * QUARTERS + q + 1)
                act.activation(y_sd[:, q, :], y_ms[:, q, :], ACT.Sqrt, bias=eps[:, :]).then_inc(y_sd_ready, 1)

            def gram_copy(g, q, later):
                act.wait_ge(z_done, g * QUARTERS + q + 1)
                if later:
                    act.wait_ge(stacked[q // 4], g * HALF_DMAS)
                act.activation(gram[:, :, SLOTS * q:SLOTS * (q + 1)], PZv[0:2 * PR].rearrange("p b c -> p c b"),
                               ACT.Copy).then_inc(gram_ready, 1)

            def x_columns(g, later):
                if later:
                    act.wait_ge(z_done, g * QUARTERS)
                act.activation(T[:, :, PR], xT[:, bass.ds(g * GROUP, GROUP)], ACT.Copy).then_inc(xcol_ready, 1)

            def before(g, step):
                if step in (1, 2):
                    gram_copy(g, QUARTERS - 3 + step, True if not isinstance(g, int) or g else False)
                if step == 2:
                    act.activation(zx[ROW_XS:ROW_XS + 1, :, :].rearrange("p h b -> p (h b)"),
                                   xs[ROW_XS:ROW_XS + 1, :, :, :].rearrange("p g h b -> p (g h b)")[
                                       :, bass.ds(g * GROUP, GROUP)], ACT.Copy).then_inc(zx_xs_ready, 1)
                if step == 6:
                    act.wait_ge(f_mv_ready, g + 1)
                    act.activation(f_sd[:, :], f_mv[:, 1:2], ACT.Sqrt, bias=eps[:, :]).then_inc(f_sd_ready, 1)
                if step == 7:
                    act.wait_ge(tz_done, g + 1)
                    for c in range(KEPT // P):
                        a = act.activation(zT[:, c, :].rearrange("p (b h) -> p h b", h=2),
                                           PM[:, P * c:P * c + P].rearrange("p (h b) -> p h b", h=2),
                                           ACT.Identity, scale=glbl[:, 0, c:c + 1], bias=glbl[:, 1, c:c + 1])
                    a.then_inc(zT_ready, 1)
                if step == 9:
                    act.wait_ge(m1_done, g + 1)
                    for m in range(H1 // P):
                        a = act.activation(h1[:, m, :], PF[:, P * m:P * m + P], ACT.Relu, bias=b1[:, m:m + 1])
                    a.then_inc(h1_ready, 1)
                if step == 10:
                    act.wait_ge(m2_done, g + 1)
                    for m in range(H2 // P):
                        a = act.activation(h2[:, m, :], PM[:, P * m:P * m + P], ACT.Relu, bias=b2[:, m:m + 1])
                    a.then_inc(h2_ready, 1)
                if step == 12:
                    act.wait_ge(m3_done, g + 1)
                    act.activation(y_row[0:1, bass.ds(g * GROUP, GROUP)], PF[0:1, 0:GROUP],
                                   ACT.Copy).then_inc(y_ready, 1)

            def group(g, later):
                embT_copy(g, 0)
                embT_copy(g, 1)
                u_spread(g, 0)
                for j in range(PAIRS):
                    if j + 2 < PAIRS:
                        embT_copy(g, j + 2)
                    for q in range(QUARTERS):
                        if LAST_PAIR[q] + 1 == j:
                            y_spread(g, q)
                    if later and j == 0:
                        y_spread(g - 1, QUARTERS - 1)
                    if j + 1 < PAIRS:
                        u_spread(g, j + 1)
                    for q in range(QUARTERS):
                        if LAST_PAIR[q] == j:
                            y_square(g, q)
                    if later:
                        before(g - 1, j)
                    elif j == 10:
                        act.wait_ge(xs_done, 1)
                        act.activation(xs[ROW_XS:ROW_XS + 1, :, :, :].rearrange("p g h b -> p g b h"),
                                       PM[0:1, :].rearrange("p (g b h) -> p g b h", g=NG, h=2),
                                       ACT.Copy).then_inc(xs_ready, 1)
                        act.wait_ge(w5_done, 1)
                        act.activation(wl5[0:ROWS_X, :], PF[0:ROWS_X, :], ACT.Copy).then_inc(wl5_ready, 1)
                        act.wait_ge(xs_ready, 1)
                    if j == 2:
                        x_columns(g, later)
                    for q in range(QUARTERS):
                        if LAST_PAIR[q] + LAG + 1 == j:
                            gram_copy(g, q, later)

            act.wait_ge(consts_ready, 3)
            act.wait_ge(x_done, 1)
            act.activation(xsq[:, :], PF[:, :], ACT.Square).then_inc(xsq_ready, 1)
            act.wait_ge(x_done, 2)
            act.activation(x_r[:, :], PM[:, :], ACT.Sqrt, bias=eps[:, :]).then_inc(x_sd_ready, 1)
            act.wait_ge(xT_ready, 1)
            act.wait_ge(consts_ready, 6)
            group(0, False)
            act.wait_ge(l_late, 16 * 11)
            with act.Fori(1, NG) as g:
                group(g, True)
            y_spread(NG - 1, QUARTERS - 1)
            for step in range(PAIRS):
                before(NG - 1, step)

        @block.vector
        def _(dve):
            steps = [0]

            def chain(ins):
                steps[0] += 1
                ins.then_inc(dve_setup, 1)
                dve.wait_ge(dve_setup, steps[0])

            def centre(w, m, n):
                chain(dve.tensor_reduce(m, w, AX_X, ALU.add))
                chain(dve.tensor_scalar(m, m, -1.0 / n, None, ALU.mult))
                bc = m.unsqueeze(2).to_broadcast([*w.shape]) if len(w.shape) == 3 else m.to_broadcast([*w.shape])
                return dve.tensor_tensor(w, w, bc, ALU.add)

            def three_parts(src, width, s0, dst):
                n = slice(0, width)
                chain(dve.tensor_copy(part[:, 0, n], src))
                chain(dve.tensor_tensor(rest[:, 0, n], src, part[:, 0, n], ALU.subtract))
                chain(dve.tensor_copy(part[:, 1, n], rest[:, 0, n]))
                chain(dve.tensor_tensor(rest[:, 1, n], rest[:, 0, n], part[:, 1, n], ALU.subtract))
                chain(dve.tensor_copy(part[:, 2, n], rest[:, 1, n]))
                chain(dve.tensor_scalar(acc9[:, n], part[:, 0, n], sel9[:, s0:s0 + 1], None, ALU.mult))
                for i in (1, 2):
                    chain(dve.scalar_tensor_tensor(out=acc9[:, n], in0=part[:, i, n], scalar=sel9[:, s0 + i:s0 + i + 1],
                                                   in1=acc9[:, n], op0=ALU.mult, op1=ALU.add))
                a = acc9[:, n]
                if len(dst.shape) == 3:
                    a = a.unsqueeze(1).to_broadcast([*dst.shape])
                return dve.tensor_copy(dst, a)

            dve.wait_ge(l_proj, 48)
            centre(wsT[:, :, :], ws_m[:, :], E).then_inc(wsT_ready, 1)
            dve.wait_ge(l_dense, 48)
            centre(wdT[:, :, :], wd_m[:, :], E).then_inc(wd_ready, 1)
            dve.wait_ge(l_comb, 64)
            centre(wsiT[:, :], wsi_m[:, :], PR).then_inc(wsi_ready, 1)
            chain(three_parts(bs9[:, :], E, 0, bias_l[:, :]))
            dve.wait_ge(sc_done, 1)
            chain(dve.tensor_copy(sc9[:, :], PZ[0:9, 0:PR]))
            three_parts(sc9[:, :], PR, 3, bias_r[:, :, :]).then_inc(bias_ready, 1)
            centre(wbd[:, :, :], wbd_m[:, :], PR).then_inc(wbd_ready, 1)
            dve.wait_ge(x_sd_ready, 1)
            chain(dve.reciprocal(x_r[:, :], x_r[:, :]))
            chain(dve.tensor_tensor(xT[:, :], PF[:, :], x_r[:, :], ALU.mult))
            dve.tensor_scalar(xT[:, :], xT[:, :], gdbd[:, 0:1], gdbd[:, 1:2], ALU.mult, ALU.add).then_inc(xT_ready, 1)

            def fold_weights():
                dve.wait_ge(l_late, 16 * 11)
                ga, gB, ba, bB = (gb[:, i, :] for i in range(4))
                chain(dve.tensor_tensor(gg[:, 0, :], ga, gB, ALU.mult))
                chain(dve.tensor_tensor(gg[:, 1, :], ga, bB, ALU.mult))
                chain(dve.tensor_tensor(gg[:, 2, :], gB, ba, ALU.mult))
                chain(dve.tensor_tensor(gg[:, 3, :], ba, bB, ALU.mult))
                chain(dve.memset(fold[:, :, :], 0.0))
                chain(dve.memset(foldx[:, :], 0.0))
                for k in range(KC):
                    to = fold[:, k, ROW_S:ROW_S + PR]
                    chain(dve.tensor_scalar(to, sel[:, 0, k, :], gg[:, 1, k:k + 1], None, ALU.mult))
                    chain(dve.scalar_tensor_tensor(out=to, in0=sel[:, 1, k, :], scalar=gg[:, 2, k:k + 1], in1=to,
                                                   op0=ALU.mult, op1=ALU.add))
                    chain(dve.tensor_scalar(fold[:, k, ROW_ONE:ROW_ONE + 1], gg[:, 3, k:k + 1], float(E), None,
                                            ALU.mult))
                chain(dve.tensor_scalar(foldx[:, 0:PR], ident[0:PR, 0:PR], gbsi[:, 0:1], None, ALU.mult))
                dve.tensor_copy(foldx[:, ROW_XS:ROW_XS + 1], gbsi[:, 1:2]).then_inc(fold_ready, 1)

            def scale_wl():
                dve.wait_ge(w5_done, 1)
                for k in range(KC):
                    a = dve.tensor_scalar(wl[:, k, :], wl[:, k, :], gg[:, 0, k:k + 1], None, ALU.mult)
                a.then_inc(wl_ready, 1)

            def project(g, j):
                dve.wait_ge(u_sd_ready, g * PAIRS + j + 1)
                dve.reciprocal(u_r[:, j, :], u_sd[:, j, :]).then_inc(u_r_ready, 1)
                dve.wait_ge(u_r_ready, g * PAIRS + j + 1)
                for i in range(2):
                    a = dve.scalar_tensor_tensor(out=proj[:, j, i, :], in0=TU[bank(j)][:, P + E * i:P + E * (i + 1)],
                                                 scalar=u_r[:, j, i:i + 1], in1=gs_b[:, :],
                                                 op0=ALU.mult, op1=ALU.mult)
                a.then_inc(proj_ready, 1)

            def y_sums(g, q):
                dve.wait_ge(ysq_ready, g * QUARTERS + q + 1)
                dve.tensor_reduce(y_ms[:, q, :], ysq[:, q % 2, :, :], AX_X, ALU.add).then_inc(y_ms_ready, 1)

            def normalise(g, q):
                dve.wait_ge(y_sd_ready, g * QUARTERS + q + 1)
                dve.reciprocal(y_r[:, q, :], y_sd[:, q, :]).then_inc(y_r_ready, 1)
                dve.wait_ge(y_r_ready, g * QUARTERS + q + 1)
                dve.tensor_tensor(T[:, QS * q:QS * (q + 1), 0:PR], PY[q % 2][:, :, :],
                                  y_r[:, q, :].unsqueeze(2).to_broadcast([P, QS, PR]), ALU.mult).then_inc(T_ready, 1)

            def before(g, step):
                if step == 5:
                    dve.wait_ge(f_done, g + 1)
                    dve.bn_stats(f_bn[:, :], PF[:, :]).then_inc(f_bn_ready, 1)
                    dve.wait_ge(f_bn_ready, g + 1)
                    dve.sem_inc(f_bn_seen, 1)
                    dve.bn_aggr(f_mv[:, :], f_bn[:, :]).then_inc(f_mv_ready, 1)
                if step == 6:
                    dve.wait_ge(f_sd_ready, g + 1)
                    dve.reciprocal(f_r[:, :], f_sd[:, :]).then_inc(f_r_ready, 1)
                    dve.wait_ge(f_r_ready, g + 1)
                    dve.tensor_scalar(znorm[:, :], PF[:, 0:KEPT], f_mv[:, 0:1], f_r[:, :],
                                      ALU.subtract, ALU.mult).then_inc(znorm_ready, 1)

            def group(g, later):
                project(g, 0)
                for j in range(PAIRS):
                    for q in range(QUARTERS):
                        if LAST_PAIR[q] + 1 == j:
                            normalise(g, q)
                    if later and j == 0:
                        normalise(g - 1, QUARTERS - 1)
                    if j + 1 < PAIRS:
                        project(g, j + 1)
                    for q in range(QUARTERS):
                        if LAST_PAIR[q] == j:
                            y_sums(g, q)
                    if later:
                        before(g - 1, j)
                    elif j == 6:
                        fold_weights()
                    elif j == 10:
                        scale_wl()

            group(0, False)
            with dve.Fori(1, NG) as g:
                group(g, True)
            normalise(NG - 1, QUARTERS - 1)
            for step in range(PAIRS):
                before(NG - 1, step)


def layouts(inputs):
    f32 = np.float32
    a = {k: np.asarray(v) for k, v in inputs.items()}
    tables = [a[f"tbl_{f}"] for f in range(NF)]
    base = np.cumsum([0] + [x.shape[0] for x in tables[:-1]]).astype(np.int32)
    row = np.arange(HALF * P)
    out = {"tables": np.concatenate(tables, axis=0)}
    out["ids"] = np.ascontiguousarray(a["ids"].reshape(NG * TILES, P).T)
    out["bases"] = np.ascontiguousarray(base[row % NF].reshape(HALF, P).T)
    out["ident"] = np.eye(P, dtype=f32)
    wsT = np.zeros((2, D, 2, E), f32)
    wsT[0, :, 0] = wsT[1, :, 1] = a["L0_rec_Ws"].T
    out["wsT"] = wsT.reshape(P, 2, E)
    out["gs"] = a["L0_rec_gs"]
    wsi = a["L0_rec_Wsi"]
    wbd = np.zeros((P, NSPAN, PR), f32)
    for k in range(HALF):
        for p in range(P):
            s, n = divmod(P * k + p, NF)
            wbd[p, AT[k] + s - span(k)[0], :] = wsi[:, n]
    out["wbd"] = wbd
    out["wsiT"] = np.ascontiguousarray(wsi.T)
    out["bs"] = a["L0_rec_bs"]
    nine = np.arange(9)[:, None]
    out["sel9"] = np.concatenate([nine // 3 == np.arange(3), nine % 3 == np.arange(3)], axis=1).astype(f32)
    out["wdT"] = np.ascontiguousarray(a["L0_rec_Wd"].T.reshape(DENSE // P, P, E).transpose(1, 0, 2))
    out["denseT"] = np.ascontiguousarray(a["r_dense_t"].T.reshape(DENSE // P, P, B).transpose(1, 0, 2))
    out["gdbd"] = np.stack([a["L0_rec_gd"], a["L0_rec_bd"]], axis=1)
    wl_in, gsi, bsi = a["L0_rec_Wl"], a["L0_rec_gsi"], a["L0_rec_bsi"]
    wl = np.zeros((P, KC, OUT), f32)
    gb = np.zeros((P, 4, KC), f32)
    sel = np.zeros((P, 2, KC, PR), f32)
    for p in range(P):
        for k in range(KC):
            i, c = gram_entry(p, k)
            if i > c:
                wl[p, k, :] = wl_in[:, (i + 1) * i // 2 + c + 1]
                gb[p, :, k] = gsi[c], gsi[i], bsi[c], bsi[i]
                sel[p, 0, k, c] = sel[p, 1, k, i] = 1
    out |= {"wl": wl, "gb": gb, "sel": sel}
    out["wlx"] = np.stack([wl_in[:, (i + 1) * i // 2] for i in range(PR)], axis=0)
    out["gbsi"] = np.stack([gsi, bsi], axis=1)
    glbl = np.stack([a["L0_rec_gl"][:KEPT], a["L0_rec_bl"][:KEPT]])
    out["glbl"] = np.ascontiguousarray(glbl.reshape(2, KEPT // P, P).transpose(2, 0, 1))
    w1 = np.concatenate([a["W_top1"][:KEPT], a["W_top1"][OUT:]], axis=0)
    out["w1"] = np.ascontiguousarray(w1.reshape(-1, P, H1).transpose(1, 0, 2))
    out["b1"] = np.ascontiguousarray(a["b_top1"].reshape(-1, P).T)
    out["w2"] = np.ascontiguousarray(a["W_top2"].reshape(-1, P, H2).transpose(1, 0, 2))
    out["b2"] = np.ascontiguousarray(a["b_top2"].reshape(-1, P).T)
    out["w3"] = np.ascontiguousarray(a["W_top3"].reshape(-1, P).T)
    return out


def kernel(**inputs):
    import concourse.bacc as bacc
    from concourse.bass_utils import run_bass_kernel_spmd

    nc = bacc.Bacc("TRN2", target_bir_lowering=False, num_devices=1)
    arrays = {f"{k}_dram": v for k, v in layouts(inputs).items()}
    t = {k[:-5]: nc.dram_tensor(k, v.shape, mybir.dt.from_np(v.dtype), kind="ExternalInput").ap()
         for k, v in arrays.items()}
    t["out"] = nc.dram_tensor("y_dram", (B, 1), F32, kind="ExternalOutput").ap()
    dlrm_tower(nc, t)
    r = run_bass_kernel_spmd(nc, [arrays], core_ids=[0])
    return r.results[0]["y_dram"]
```

```python
from contextlib import ExitStack

import numpy as np
import concourse.bass as bass
from concourse import mybir

ALU = mybir.AluOpType
ACT = mybir.ActivationFunctionType
AX_X = mybir.AxisListType.X
F32 = mybir.dt.float32
BF16 = mybir.dt.bfloat16
I32 = mybir.dt.int32

P = 128
EPS = 1e-5
B = 512
NF = 26
D = 64
E = 128
PR = 32
DENSE = 256
OUT = 512
KEPT = 384
H1 = 512
H2 = 256

GROUP = 128
NG = B // GROUP
TILES = GROUP * NF // P
PAIRS = TILES // 2
HALF = TILES // 2
QS = 16
QUARTERS = GROUP // QS
ITEMS = PR + 2
SLOTS = QS // 2
NZ = GROUP // 2
KC = PR // 8
ROW_ONE, ROW_S, ROW_XS = 32, 64, 96
ROWS_X = ROW_XS + 1


def span(tile):
    k = tile % HALF
    return P * k // NF, (P * k + P - 1) // NF


SPANS = [span(k)[1] - span(k)[0] + 1 for k in range(HALF)]
AT = [sum(SPANS[:k]) for k in range(HALF)]
NSPAN = sum(SPANS)


def pieces(tile):
    lo, hi = span(tile)
    base = (tile // HALF) * (HALF * P // NF)
    out = []
    for q in range(QUARTERS):
        a, b = max(base + lo, QS * q), min(base + hi, QS * q + QS - 1)
        if a <= b:
            out.append((q, (a - QS * q) * PR, (b - a + 1) * PR, (AT[tile % HALF] + a - base - lo) * PR))
    return out


LAST_PAIR = [((QS * NF * (q + 1) - 1) // P) // 2 for q in range(QUARTERS)]
FIRST_TILE = [QS * NF * q // P for q in range(QUARTERS)]
LAG = 2


def gram_entry(p, k):
    i, c = p % PR, 4 * k + p // PR
    return None if i == c else (i, c) if i > c else (PR - 1 - i, PR - 1 - c)


NTU, NPY = 3, 3


def wait_if_any(eng, semaphore, value):
    if value > 0:
        eng.wait_ge(semaphore, value)


def dlrm_tower(nc, t):
    ctx = ExitStack()
    with ctx:
        def sb(name, shape, dt=F32):
            return ctx.enter_context(nc.sbuf_tensor(name, shape, dt))

        def pb(name, shape):
            return ctx.enter_context(nc.psum_tensor(name, shape, F32))

        def sem(name):
            return ctx.enter_context(nc.semaphore(name))

        ids = sb("ids_sb", [P, NG * TILES], I32)
        bases = sb("bases_sb", [P, HALF], I32)
        rows_at = sb("rows_at", [P, 2, HALF], I32)
        emb = sb("emb", [P, TILES, D])
        embT = sb("embT", [P, PAIRS, P])
        proj = sb("proj", [P, PAIRS, 2, E])
        junk = sb("junk", [P, 2, E])
        u_ms = sb("u_ms", [P, PAIRS, 2])
        u_sd = sb("u_sd", [P, PAIRS, 2])
        u_r = sb("u_r", [P, PAIRS, 2])
        ysq = sb("ysq", [P, 2, QS, PR])
        y_ms = sb("y_ms", [P, QUARTERS, QS])
        y_sd = sb("y_sd", [P, QUARTERS, QS])
        y_r = sb("y_r", [P, QUARTERS, QS])
        T = sb("T", [P, GROUP, ITEMS])
        gram = sb("gram", [2 * PR, ITEMS, NZ])
        zn = sb("zn", [P, KC, 2, NZ])
        zr = sb("zr", [P, KC, 2, NZ])
        zx = sb("zx", [P, 2, NZ])
        f_bn = sb("f_bn", [P, 6])
        f_mv = sb("f_mv", [P, 2])
        f_sd = sb("f_sd", [P, 1])
        f_r = sb("f_r", [P, 1])
        znorm = sb("znorm", [P, KEPT])
        zT = sb("zT", [P, KEPT // P, GROUP])
        h1 = sb("h1", [P, H1 // P, GROUP])
        h2 = sb("h2", [P, H2 // P, GROUP])
        y_row = sb("y_row", [1, B])
        wbd = sb("wbd", [P, NSPAN, PR])
        wbd_m = sb("wbd_m", [P, NSPAN])
        wsT = sb("wsT", [P, 2, E])
        ws_m = sb("ws_m", [P, 2])
        gs_b = sb("gs_b", [P, E])
        wsiT = sb("wsiT", [NF, PR])
        wsi_m = sb("wsi_m", [NF, 1])
        bs9 = sb("bs9", [9, E])
        sel9 = sb("sel9", [9, 6])
        sc9 = sb("sc9", [9, PR])
        part = sb("part", [9, 3, E], BF16)
        rest = sb("rest", [9, 2, E])
        acc9 = sb("acc9", [9, E])
        bias_l = sb("bias_l", [9, E], BF16)
        bias_r = sb("bias_r", [9, QS, PR], BF16)
        wdT = sb("wdT", [P, DENSE // P, E])
        wd_m = sb("wd_m", [P, DENSE // P])
        denseT = sb("denseT", [P, DENSE // P, B])
        gdbd = sb("gdbd", [P, 2])
        xsq = sb("xsq", [P, B])
        x_r = sb("x_r", [P, B])
        xT = sb("xT", [P, B])
        xs = sb("xs", [P, NG, 2, NZ])
        wl = sb("wl", [P, KC, OUT])
        wlx = sb("wlx", [PR, OUT])
        wl5 = sb("wl5", [P, OUT])
        gb = sb("gb", [P, 4, KC])
        gg = sb("gg", [P, 4, KC])
        sel = sb("sel", [P, 2, KC, PR])
        fold = sb("fold", [P, KC, ROWS_X])
        foldx = sb("foldx", [PR, ROWS_X])
        gbsi = sb("gbsi", [PR, 2])
        mask = sb("mask", [P, KC], I32)
        glbl = sb("glbl", [P, 2, KEPT // P])
        w1 = sb("w1", [P, (KEPT + DENSE) // P, H1])
        b1 = sb("b1", [P, H1 // P])
        w2 = sb("w2", [P, H1 // P, H2])
        b2 = sb("b2", [P, H2 // P])
        w3 = sb("w3", [P, H2 // P])
        ident = sb("ident", [P, P])
        ones = sb("ones", [P, 9])
        mean_w = sb("mean_w", [P, P])
        eps = sb("eps", [P, 1])

        TU = [pb(f"tu{i}", [P, 512]) for i in range(NTU)]
        PY = [pb(f"py{i}", [P, QS, PR]) for i in range(NPY)]
        PZ = pb("pz", [P, 512])
        PZv = PZ[:, 0:SLOTS * ITEMS].rearrange("p (b c) -> p b c", c=ITEMS)
        PF = pb("pf", [P, 512])

        l_ids = sem("l_ids")
        l_proj = sem("l_proj")
        l_comb = sem("l_comb")
        l_dense = sem("l_dense")
        l_late = sem("l_late")
        rows_ready = sem("rows_ready")
        rows_seen = sem("rows_seen")
        gathered = [sem(f"gathered{j}") for j in range(PAIRS)]
        consts_ready = sem("consts_ready")
        t_done = sem("t_done")
        u_done = sem("u_done")
        y_done = sem("y_done")
        z_done = sem("z_done")
        f_done = sem("f_done")
        tz_done = sem("tz_done")
        m1_done = sem("m1_done")
        m2_done = sem("m2_done")
        m3_done = sem("m3_done")
        x_done = sem("x_done")
        sc_done = sem("sc_done")
        sc_ready = sem("sc_ready")
        xs_done = sem("xs_done")
        w5_done = sem("w5_done")
        embT_ready = sem("embT_ready")
        u_ms_ready = sem("u_ms_ready")
        u_sd_ready = sem("u_sd_ready")
        ysq_ready = sem("ysq_ready")
        y_sd_ready = sem("y_sd_ready")
        xcol_ready = sem("xcol_ready")
        gram_ready = sem("gram_ready")
        f_sd_ready = sem("f_sd_ready")
        zT_ready = sem("zT_ready")
        h1_ready = sem("h1_ready")
        h2_ready = sem("h2_ready")
        y_ready = sem("y_ready")
        xsq_ready = sem("xsq_ready")
        x_sd_ready = sem("x_sd_ready")
        xs_ready = sem("xs_ready")
        zx_xs_ready = sem("zx_xs_ready")
        wl5_ready = sem("wl5_ready")
        dve_setup = sem("dve_setup")
        wsT_ready = sem("wsT_ready")
        wbd_ready = sem("wbd_ready")
        wsi_ready = sem("wsi_ready")
        wd_ready = sem("wd_ready")
        bias_ready = sem("bias_ready")
        xT_ready = sem("xT_ready")
        wl_ready = sem("wl_ready")
        fold_ready = sem("fold_ready")
        u_r_ready = sem("u_r_ready")
        proj_ready = sem("proj_ready")
        y_ms_ready = sem("y_ms_ready")
        y_r_ready = sem("y_r_ready")
        T_ready = sem("T_ready")
        f_bn_ready = sem("f_bn_ready")
        f_bn_seen = sem("f_bn_seen")
        f_mv_ready = sem("f_mv_ready")
        f_r_ready = sem("f_r_ready")
        znorm_ready = sem("znorm_ready")
        stacked = sem("stacked")
        turned = sem("turned")
        merged = sem("merged")
        stored = sem("stored")

        block = ctx.enter_context(nc.Block())

        @block.sync
        def _(sp):
            sp.dma_start(ids[:, :], t["ids"]).then_inc(l_ids, 16)
            sp.dma_start(bases[:, :], t["bases"]).then_inc(l_ids, 16)
            sp.dma_start(ident[:, :], t["ident"]).then_inc(l_proj, 16)
            sp.dma_start(wsT[:, :, :], t["wsT"]).then_inc(l_proj, 16)
            sp.dma_start(gs_b[:, :], t["gs"].partition_broadcast(P)).then_inc(l_proj, 16)
            sp.dma_start(wdT[:, :, :], t["wdT"]).then_inc(l_dense, 16)
            sp.dma_start(denseT[:, :, :], t["denseT"]).then_inc(l_dense, 16)
            sp.dma_start(gdbd[:, :], t["gdbd"]).then_inc(l_dense, 16)
            for dst, src in ((wl, "wl"), (wlx, "wlx"), (gb, "gb"), (sel, "sel"), (gbsi, "gbsi"), (mask, "mask"),
                             (glbl, "glbl"), (w1, "w1"), (b1, "b1"), (w2, "w2"), (b2, "b2"), (w3, "w3")):
                sp.dma_start(dst[tuple(slice(None) for _ in dst.shape)], t[src]).then_inc(l_late, 16)

            sp.wait_ge(y_ready, NG)
            sp.dma_start(t["out"].rearrange("b one -> one b"), y_row[:, :]).then_inc(stored, 16)
            sp.wait_ge(stored, 16)

        @block.gpsimd
        def _(pool):
            pool.memset(eps[:, :], EPS).then_inc(consts_ready, 1)
            pool.memset(mean_w[:, :], 1.0 / E).then_inc(consts_ready, 1)
            pool.memset(ones[:, :], 1.0).then_inc(consts_ready, 1)
            pool.wait_ge(l_ids, 32)

            def gather_half(g, half, later):
                if later:
                    pool.wait_ge(t_done, (g - 1) * PAIRS + (HALF + 1) // 2 + half * (HALF // 2))
                pool.tensor_tensor(rows_at[:, half, :], ids[:, bass.ds(g * TILES + half * HALF, HALF)],
                                   bases[:, :], ALU.add).then_inc(rows_ready, 1)
                pool.wait_ge(rows_ready, g * 2 + half + 1)
                pool.sem_inc(rows_seen, 1)
                for k in range(half * HALF, (half + 1) * HALF):
                    pool.indirect_dma_start(
                        emb[:, k, :], None, t["tables"],
                        bass.IndirectOffsetOnAxis(ap=rows_at[:, half, k - half * HALF:k - half * HALF + 1], axis=0),
                    ).then_inc(gathered[k // 2], 16)

            gather_half(0, 0, False)
            pool.memset(zx[:, :, :], 0.0).then_inc(consts_ready, 1)
            pool.wait_ge(consts_ready, 4)
            pool.memset(T[:, :, PR + 1:PR + 2], 1.0).then_inc(consts_ready, 1)
            pool.wait_ge(consts_ready, 5)
            pool.memset(zx[ROW_ONE:ROW_ONE + 1, :, :], 1.0).then_inc(consts_ready, 1)
            pool.wait_ge(consts_ready, 6)
            gather_half(0, 1, False)
            for g in range(1, NG):
                gather_half(g, 0, True)
                gather_half(g, 1, True)

        @block.tensor
        def _(pe):
            def transposes(g, j):
                pe.wait_ge(gathered[j], g * 32 + 32)
                wait_if_any(pe, proj_ready, g * PAIRS + j + 1 - NTU)
                pe.transpose(TU[(PAIRS * g + j) % NTU][:, 0:P], emb[:, 2 * j:2 * j + 2, :].rearrange("p t d -> p (t d)"),
                             ident[:, :]).then_inc(t_done, 1)

            def project(g, j):
                pe.wait_ge(embT_ready, g * PAIRS + j + 1)
                pe.matmul(TU[(PAIRS * g + j) % NTU][:, P:P + 2 * E], embT[:, j, :], wsT[:, :, :].rearrange("p t e -> p (t e)"),
                          start=True, stop=True).then_inc(u_done, 1)

            def combine(g, j):
                pe.wait_ge(proj_ready, g * PAIRS + j + 1)
                for tile in (2 * j, 2 * j + 1):
                    for q, col, n, at in pieces(tile):
                        if tile == FIRST_TILE[q]:
                            wait_if_any(pe, T_ready, g * QUARTERS + q + 1 - NPY)
                            pe.matmul(PY[(QUARTERS * g + q) % NPY][:, :, :].rearrange("p b c -> p (b c)"), bias_l[:, :],
                                      bias_r[:, :, :].rearrange("p b c -> p (b c)"),
                                      start=True, stop=False, skip_group_check=True)
                        mm = pe.matmul(PY[(QUARTERS * g + q) % NPY][:, :, :].rearrange("p b c -> p (b c)")[:, col:col + n],
                                       proj[:, j, tile % 2, :],
                                       wbd[:, :, :].rearrange("p b c -> p (b c)")[:, at:at + n],
                                       start=False, stop=col + n == QS * PR, skip_group_check=True)
                mm.then_inc(y_done, 1)

            def gram_products(g, q):
                pe.wait_ge(T_ready, g * QUARTERS + q + 1)
                if q == 0:
                    pe.wait_ge(xcol_ready, g + 1)
                wait_if_any(pe, gram_ready, g * QUARTERS + q)
                for s in range(QS):
                    h, b = s % 2, s // 2
                    of = T[:, QS * q + s, 0:ITEMS]
                    mm = pe.matmul(PZ[PR * h:PR * h + PR, ITEMS * b:ITEMS * (b + 1)], of[:, 0:PR], of,
                                   start=True, stop=True)
                mm.then_inc(z_done, 1)

            def flat_layer(g):
                pe.wait_ge(merged, g + 1)
                pe.wait_ge(zx_xs_ready, g + 1)
                wait_if_any(pe, y_ready, g)
                for k in range(KC):
                    pe.matmul(PF[:, :], zn[:, k, :, :].rearrange("p h b -> p (h b)"), wl[:, k, :],
                              start=(k == 0), stop=False)
                pe.matmul(PF[:, :], zx[0:ROWS_X, :, :].rearrange("p h b -> p (h b)"), wl5[0:ROWS_X, :],
                          start=False, stop=True).then_inc(f_done, 1)

            def z_transposes(g):
                pe.wait_ge(znorm_ready, g + 1)
                for c in range(KEPT // P):
                    mm = pe.transpose(PF[:, P * c:P * c + P], znorm[:, P * c:P * c + P], ident[:, :])
                mm.then_inc(tz_done, 1)

            def mlp1(g):
                pe.wait_ge(zT_ready, g + 1)
                for m in range(H1 // P):
                    for n, c in enumerate((3, 4, 0, 1, 2)):
                        rhs = zT[:, c, :] if c < 3 else denseT[:, c - 3, bass.ds(g * GROUP, GROUP)]
                        mm = pe.matmul(PF[:, P * m:P * m + P], w1[:, c, P * m:P * m + P], rhs,
                                       start=(n == 0), stop=(n == 4))
                mm.then_inc(m1_done, 1)

            def mlp2(g):
                pe.wait_ge(h1_ready, g + 1)
                for m in range(H2 // P):
                    for c in range(H1 // P):
                        mm = pe.matmul(PF[:, P * m:P * m + P], w2[:, c, P * m:P * m + P], h1[:, c, :],
                                       start=(c == 0), stop=(c == H1 // P - 1))
                mm.then_inc(m2_done, 1)

            def mlp3(g):
                pe.wait_ge(h2_ready, g + 1)
                for c in range(H2 // P):
                    mm = pe.matmul(PF[0:1, 0:GROUP], w3[:, c:c + 1], h2[:, c, :],
                                   start=(c == 0), stop=(c == H2 // P - 1))
                mm.then_inc(m3_done, 1)

            def before(g, step):
                if step == 3:
                    flat_layer(g)
                if step == 5:
                    z_transposes(g)
                if step == 6:
                    mlp1(g)
                if step == 8:
                    mlp2(g)
                if step == 9:
                    mlp3(g)

            def x_projected():
                pe.wait_ge(wd_ready, 1)
                for c in range(DENSE // P):
                    mm = pe.matmul(PF[:, :], wdT[:, c, :], denseT[:, c, :], start=(c == 0), stop=(c == 1))
                mm.then_inc(x_done, 1)

            def bias_sums():
                pe.wait_ge(wsi_ready, 1)
                pe.matmul(PZ[0:9, 0:PR], ones[0:NF, :], wsiT[:, :], start=True, stop=True).then_inc(sc_done, 1)

            def x_variance():
                pe.wait_ge(xsq_ready, 1)
                pe.wait_ge(sc_ready, 1)
                pe.matmul(PZ[:, :], mean_w[:, :], xsq[:, :], start=True, stop=True).then_inc(x_done, 1)

            def x_sums():
                pe.wait_ge(xT_ready, 1)
                pe.matmul(PF[0:1, :], ones[:, 0:1], xT[:, :], start=True, stop=True).then_inc(xs_done, 1)

            def folded_weights():
                pe.wait_ge(fold_ready, 1)
                pe.wait_ge(xs_ready, 1)
                for k in range(KC):
                    pe.matmul(PF[0:ROWS_X, :], fold[:, k, :], wl[:, k, :], start=(k == 0), stop=False)
                pe.matmul(PF[0:ROWS_X, :], foldx[:, :], wlx[:, :], start=False, stop=True).then_inc(w5_done, 1)

            def group(g):
                for j in range(PAIRS):
                    combine(g, j)
                    if g * PAIRS + j + 2 < NG * PAIRS:
                        project(*divmod(g * PAIRS + j + 2, PAIRS))
                    if g * PAIRS + j + 3 < NG * PAIRS:
                        transposes(*divmod(g * PAIRS + j + 3, PAIRS))
                    if g:
                        before(g - 1, j)
                    elif j == 1:
                        x_sums()
                    elif j == 7:
                        folded_weights()
                    for q in range(QUARTERS):
                        if LAST_PAIR[q] + 1 == j:
                            gram_products(g, q)
                    if g and j == 0:
                        gram_products(g - 1, QUARTERS - 1)

            pe.wait_ge(consts_ready, 3)
            pe.wait_ge(l_proj, 48)
            bias_sums()
            x_projected()
            transposes(0, 0)
            transposes(0, 1)
            pe.wait_ge(wsT_ready, 1)
            project(0, 0)
            x_variance()
            transposes(0, 2)
            project(0, 1)
            pe.wait_ge(bias_ready, 1)
            pe.wait_ge(wbd_ready, 1)
            for g in range(NG):
                if g == 1:
                    pe.wait_ge(wl5_ready, 1)
                    pe.wait_ge(wl_ready, 1)
                group(g)
            gram_products(NG - 1, QUARTERS - 1)
            for step in range(PAIRS):
                before(NG - 1, step)

        @block.scalar
        def _(act):
            act.dma_start(wbd[:, :, :], t["wbd"]).then_inc(l_comb, 16)
            act.dma_start(wsiT[:, :], t["wsiT"]).then_inc(l_comb, 16)
            act.dma_start(bs9[:, :], t["bs"].partition_broadcast(9)).then_inc(l_comb, 16)
            act.dma_start(sel9[:, :], t["sel9"]).then_inc(l_comb, 16)

            def embT_copy(g, j):
                act.wait_ge(t_done, g * PAIRS + j + 1)
                act.activation(embT[:, j, :], TU[(PAIRS * g + j) % NTU][:, 0:P], ACT.Copy).then_inc(embT_ready, 1)

            def u_spread(g, j):
                act.wait_ge(u_done, g * PAIRS + j + 1)
                for i in range(2):
                    a = act.activation(junk[:, i, :], TU[(PAIRS * g + j) % NTU][:, P + E * i:P + E * (i + 1)], ACT.Square,
                                       scale=float(E) ** -0.5, accum_out=u_ms[:, j, i:i + 1])
                a.then_inc(u_ms_ready, 1)
                act.wait_ge(u_ms_ready, g * PAIRS + j + 1)
                act.activation(u_sd[:, j, :], u_ms[:, j, :], ACT.Sqrt, bias=eps[:, :]).then_inc(u_sd_ready, 1)

            def y_square(g, q):
                act.wait_ge(y_done, g * PAIRS + LAST_PAIR[q] + 1)
                act.activation(ysq[:, q % 2, :, :], PY[(QUARTERS * g + q) % NPY][:, :, :], ACT.Square,
                               scale=float(PR) ** -0.5).then_inc(ysq_ready, 1)

            def y_spread(g, q):
                act.wait_ge(y_ms_ready, g * QUARTERS + q + 1)
                act.activation(y_sd[:, q, :], y_ms[:, q, :], ACT.Sqrt, bias=eps[:, :]).then_inc(y_sd_ready, 1)

            def gram_copy(g, q):
                act.wait_ge(z_done, g * QUARTERS + q + 1)
                wait_if_any(act, stacked, g)
                act.activation(gram[:, :, SLOTS * q:SLOTS * (q + 1)], PZv[0:2 * PR].rearrange("p b c -> p c b"),
                               ACT.Copy).then_inc(gram_ready, 1)

            def x_columns(g):
                wait_if_any(act, z_done, g * QUARTERS)
                act.activation(T[:, :, PR], xT[:, bass.ds(g * GROUP, GROUP)], ACT.Copy).then_inc(xcol_ready, 1)

            def before(g, step):
                if step == 1:
                    gram_copy(g, QUARTERS - 1)
                    wait_if_any(act, f_done, g)
                    act.activation(zx[ROW_XS:ROW_XS + 1, :, :].rearrange("p h b -> p (h b)"),
                                   xs[ROW_XS:ROW_XS + 1, g, :, :].rearrange("p h b -> p (h b)"),
                                   ACT.Copy).then_inc(zx_xs_ready, 1)
                if step == 4:
                    act.wait_ge(f_mv_ready, g + 1)
                    act.activation(f_sd[:, :], f_mv[:, 1:2], ACT.Sqrt, bias=eps[:, :]).then_inc(f_sd_ready, 1)
                if step == 5:
                    act.wait_ge(tz_done, g + 1)
                    for c in range(KEPT // P):
                        a = act.activation(zT[:, c, :].rearrange("p (b h) -> p h b", h=2),
                                           PF[:, P * c:P * c + P].rearrange("p (h b) -> p h b", h=2),
                                           ACT.Identity, scale=glbl[:, 0, c:c + 1], bias=glbl[:, 1, c:c + 1])
                    a.then_inc(zT_ready, 1)
                if step == 7:
                    act.wait_ge(m1_done, g + 1)
                    for m in range(H1 // P):
                        a = act.activation(h1[:, m, :], PF[:, P * m:P * m + P], ACT.Relu, bias=b1[:, m:m + 1])
                    a.then_inc(h1_ready, 1)
                if step == 8:
                    act.wait_ge(m2_done, g + 1)
                    for m in range(H2 // P):
                        a = act.activation(h2[:, m, :], PF[:, P * m:P * m + P], ACT.Relu, bias=b2[:, m:m + 1])
                    a.then_inc(h2_ready, 1)
                if step == 10:
                    act.wait_ge(m3_done, g + 1)
                    act.activation(y_row[0:1, bass.ds(g * GROUP, GROUP)], PF[0:1, 0:GROUP],
                                   ACT.Copy).then_inc(y_ready, 1)

            def group(g):
                for j in range(PAIRS):
                    for q in range(QUARTERS):
                        if LAST_PAIR[q] + 2 == j:
                            gram_copy(g, q)
                    if g and j == 0:
                        gram_copy(g - 1, QUARTERS - 2)
                    for q in range(QUARTERS):
                        if LAST_PAIR[q] == j:
                            y_square(g, q)
                    if g * PAIRS + j + 2 < NG * PAIRS:
                        u_spread(*divmod(g * PAIRS + j + 2, PAIRS))
                    if g * PAIRS + j + 3 < NG * PAIRS:
                        embT_copy(*divmod(g * PAIRS + j + 3, PAIRS))
                    for q in range(QUARTERS):
                        if LAST_PAIR[q] == j:
                            y_spread(g, q)
                    if g:
                        before(g - 1, j)
                    elif j == 4:
                        act.wait_ge(xs_done, 1)
                        act.activation(xs[ROW_XS:ROW_XS + 1, :, :, :].rearrange("p g h b -> p g b h"),
                                       PF[0:1, :].rearrange("p (g b h) -> p g b h", g=NG, h=2),
                                       ACT.Copy).then_inc(xs_ready, 1)
                    elif j == 9:
                        act.wait_ge(w5_done, 1)
                        act.activation(wl5[0:ROWS_X, :], PF[0:ROWS_X, :], ACT.Copy).then_inc(wl5_ready, 1)
                    if j == 1:
                        x_columns(g)

            act.wait_ge(consts_ready, 3)
            act.wait_ge(x_done, 1)
            act.activation(xsq[:, :], PF[:, :], ACT.Square).then_inc(xsq_ready, 1)
            embT_copy(0, 0)
            embT_copy(0, 1)
            u_spread(0, 0)
            act.wait_ge(x_done, 2)
            act.activation(x_r[:, :], PZ[:, :], ACT.Sqrt, bias=eps[:, :]).then_inc(x_sd_ready, 1)
            embT_copy(0, 2)
            u_spread(0, 1)
            act.wait_ge(xT_ready, 1)
            act.wait_ge(consts_ready, 6)
            for g in range(NG):
                if g == 1:
                    act.wait_ge(l_late, 16 * 12)
                group(g)
            for step in range(PAIRS):
                if step == 0:
                    gram_copy(NG - 1, QUARTERS - 2)
                before(NG - 1, step)

        @block.vector
        def _(dve):
            steps = [0]

            def chain(ins):
                steps[0] += 1
                ins.then_inc(dve_setup, 1)
                dve.wait_ge(dve_setup, steps[0])

            def centre(w, m, n):
                chain(dve.tensor_reduce(m, w, AX_X, ALU.add))
                chain(dve.tensor_scalar(m, m, -1.0 / n, None, ALU.mult))
                bc = m.unsqueeze(2).to_broadcast([*w.shape]) if len(w.shape) == 3 else m.to_broadcast([*w.shape])
                return dve.tensor_tensor(w, w, bc, ALU.add)

            def three_parts(src, width, s0, dst):
                n = slice(0, width)
                chain(dve.tensor_copy(part[:, 0, n], src))
                chain(dve.tensor_tensor(rest[:, 0, n], src, part[:, 0, n], ALU.subtract))
                chain(dve.tensor_copy(part[:, 1, n], rest[:, 0, n]))
                chain(dve.tensor_tensor(rest[:, 1, n], rest[:, 0, n], part[:, 1, n], ALU.subtract))
                chain(dve.tensor_copy(part[:, 2, n], rest[:, 1, n]))
                chain(dve.tensor_scalar(acc9[:, n], part[:, 0, n], sel9[:, s0:s0 + 1], None, ALU.mult))
                for i in (1, 2):
                    chain(dve.scalar_tensor_tensor(out=acc9[:, n], in0=part[:, i, n], scalar=sel9[:, s0 + i:s0 + i + 1],
                                                   in1=acc9[:, n], op0=ALU.mult, op1=ALU.add))
                a = acc9[:, n]
                if len(dst.shape) == 3:
                    a = a.unsqueeze(1).to_broadcast([*dst.shape])
                return dve.tensor_copy(dst, a)

            dve.wait_ge(l_proj, 48)
            centre(wsT[:, :, :], ws_m[:, :], E).then_inc(wsT_ready, 1)
            dve.wait_ge(l_comb, 64)
            centre(wsiT[:, :], wsi_m[:, :], PR).then_inc(wsi_ready, 1)
            dve.wait_ge(l_dense, 48)
            centre(wdT[:, :, :], wd_m[:, :], E).then_inc(wd_ready, 1)
            chain(three_parts(bs9[:, :], E, 0, bias_l[:, :]))
            dve.wait_ge(sc_done, 1)
            dve.tensor_copy(sc9[:, :], PZ[0:9, 0:PR]).then_inc(sc_ready, 1)
            dve.wait_ge(sc_ready, 1)
            three_parts(sc9[:, :], PR, 3, bias_r[:, :, :]).then_inc(bias_ready, 1)
            centre(wbd[:, :, :], wbd_m[:, :], PR).then_inc(wbd_ready, 1)
            dve.wait_ge(x_sd_ready, 1)
            chain(dve.reciprocal(x_r[:, :], x_r[:, :]))
            chain(dve.tensor_tensor(xT[:, :], PF[:, :], x_r[:, :], ALU.mult))
            dve.tensor_scalar(xT[:, :], xT[:, :], gdbd[:, 0:1], gdbd[:, 1:2], ALU.mult, ALU.add).then_inc(xT_ready, 1)

            def fold_weights():
                dve.wait_ge(l_late, 16 * 12)
                ga, gB, ba, bB = (gb[:, i, :] for i in range(4))
                chain(dve.tensor_tensor(gg[:, 0, :], ga, gB, ALU.mult))
                chain(dve.tensor_tensor(gg[:, 1, :], ga, bB, ALU.mult))
                chain(dve.tensor_tensor(gg[:, 2, :], gB, ba, ALU.mult))
                chain(dve.tensor_tensor(gg[:, 3, :], ba, bB, ALU.mult))
                chain(dve.memset(fold[:, :, :], 0.0))
                chain(dve.memset(foldx[:, :], 0.0))
                for k in range(KC):
                    to = fold[:, k, ROW_S:ROW_S + PR]
                    chain(dve.tensor_scalar(to, sel[:, 0, k, :], gg[:, 1, k:k + 1], None, ALU.mult))
                    chain(dve.scalar_tensor_tensor(out=to, in0=sel[:, 1, k, :], scalar=gg[:, 2, k:k + 1], in1=to,
                                                   op0=ALU.mult, op1=ALU.add))
                    chain(dve.tensor_scalar(fold[:, k, ROW_ONE:ROW_ONE + 1], gg[:, 3, k:k + 1], float(E), None,
                                            ALU.mult))
                chain(dve.tensor_scalar(foldx[:, 0:PR], ident[0:PR, 0:PR], gbsi[:, 0:1], None, ALU.mult))
                dve.tensor_copy(foldx[:, ROW_XS:ROW_XS + 1], gbsi[:, 1:2]).then_inc(fold_ready, 1)

            def scale_wl():
                dve.wait_ge(w5_done, 1)
                for k in range(KC):
                    a = dve.tensor_scalar(wl[:, k, :], wl[:, k, :], gg[:, 0, k:k + 1], None, ALU.mult)
                a.then_inc(wl_ready, 1)

            def project(g, j):
                dve.wait_ge(u_sd_ready, g * PAIRS + j + 1)
                dve.reciprocal(u_r[:, j, :], u_sd[:, j, :]).then_inc(u_r_ready, 1)
                dve.wait_ge(u_r_ready, g * PAIRS + j + 1)
                for i in range(2):
                    a = dve.scalar_tensor_tensor(out=proj[:, j, i, :], in0=TU[(PAIRS * g + j) % NTU][:, P + E * i:P + E * (i + 1)],
                                                 scalar=u_r[:, j, i:i + 1], in1=gs_b[:, :],
                                                 op0=ALU.mult, op1=ALU.mult)
                a.then_inc(proj_ready, 1)

            def y_sums(g, q):
                dve.wait_ge(ysq_ready, g * QUARTERS + q + 1)
                dve.tensor_reduce(y_ms[:, q, :], ysq[:, q % 2, :, :], AX_X, ALU.add).then_inc(y_ms_ready, 1)

            def normalise(g, q):
                dve.wait_ge(y_sd_ready, g * QUARTERS + q + 1)
                dve.reciprocal(y_r[:, q, :], y_sd[:, q, :]).then_inc(y_r_ready, 1)
                dve.wait_ge(y_r_ready, g * QUARTERS + q + 1)
                dve.tensor_tensor(T[:, QS * q:QS * (q + 1), 0:PR], PY[(QUARTERS * g + q) % NPY][:, :, :],
                                  y_r[:, q, :].unsqueeze(2).to_broadcast([P, QS, PR]), ALU.mult).then_inc(T_ready, 1)

            def stack(g):
                dve.wait_ge(gram_ready, g * QUARTERS + QUARTERS)
                wait_if_any(dve, f_done, g)
                for h in range(2):
                    of = gram[PR * h:PR * h + PR, :, :]
                    for r in range(4):
                        dve.tensor_copy(zn[PR * r:PR * r + PR, :, h, :], of[:, r:PR // 2:4, :])
                        dve.tensor_copy(zr[PR * r:PR * r + PR, :, h, :], of[:, PR - 1 - r:PR // 2 - 1:-4, :])
                    dve.tensor_copy(zx[0:PR, h, :], of[:, PR, :])
                    a = dve.tensor_copy(zx[ROW_S:ROW_S + PR, h, :], of[:, PR + 1, :])
                a.then_inc(stacked, 1)
                dve.wait_ge(stacked, g + 1)
                flat = zr[:, :, :, :].rearrange("p k h b -> p (k h b)")
                dve.stream_shuffle(flat, flat, [PR - 1 - i for i in range(PR)]).then_inc(turned, 1)
                dve.wait_ge(turned, g + 1)
                dve.copy_predicated(zn[:, :, :, :].rearrange("p k h b -> p k (h b)"),
                                    mask[:, :].unsqueeze(2).to_broadcast([P, KC, GROUP]),
                                    zr[:, :, :, :].rearrange("p k h b -> p k (h b)")).then_inc(merged, 1)

            def before(g, step):
                if step == 2:
                    stack(g)
                if step == 3:
                    dve.wait_ge(f_done, g + 1)
                    dve.bn_stats(f_bn[:, :], PF[:, :]).then_inc(f_bn_ready, 1)
                    dve.wait_ge(f_bn_ready, g + 1)
                    dve.sem_inc(f_bn_seen, 1)
                    dve.bn_aggr(f_mv[:, :], f_bn[:, :]).then_inc(f_mv_ready, 1)
                if step == 4:
                    dve.wait_ge(f_sd_ready, g + 1)
                    dve.reciprocal(f_r[:, :], f_sd[:, :]).then_inc(f_r_ready, 1)
                    dve.wait_ge(f_r_ready, g + 1)
                    dve.tensor_scalar(znorm[:, :], PF[:, 0:KEPT], f_mv[:, 0:1], f_r[:, :],
                                      ALU.subtract, ALU.mult).then_inc(znorm_ready, 1)

            def group(g):
                for j in range(PAIRS):
                    for q in range(QUARTERS):
                        if LAST_PAIR[q] == j:
                            y_sums(g, q)
                    if g * PAIRS + j + 2 < NG * PAIRS:
                        project(*divmod(g * PAIRS + j + 2, PAIRS))
                    for q in range(QUARTERS):
                        if LAST_PAIR[q] == j:
                            normalise(g, q)
                    if g:
                        before(g - 1, j)
                    elif j == 4:
                        fold_weights()
                    elif j == 9:
                        scale_wl()

            project(0, 0)
            project(0, 1)
            for g in range(NG):
                group(g)
            for step in range(PAIRS):
                before(NG - 1, step)


def layouts(inputs):
    f32 = np.float32
    a = {k: np.asarray(v) for k, v in inputs.items()}
    tables = [a[f"tbl_{f}"] for f in range(NF)]
    base = np.cumsum([0] + [x.shape[0] for x in tables[:-1]]).astype(np.int32)
    row = np.arange(HALF * P)
    out = {"tables": np.concatenate(tables, axis=0)}
    out["ids"] = np.ascontiguousarray(a["ids"].reshape(NG * TILES, P).T)
    out["bases"] = np.ascontiguousarray(base[row % NF].reshape(HALF, P).T)
    out["ident"] = np.eye(P, dtype=f32)
    wsT = np.zeros((2, D, 2, E), f32)
    wsT[0, :, 0] = wsT[1, :, 1] = a["L0_rec_Ws"].T
    out["wsT"] = wsT.reshape(P, 2, E)
    out["gs"] = a["L0_rec_gs"]
    wsi = a["L0_rec_Wsi"]
    wbd = np.zeros((P, NSPAN, PR), f32)
    for k in range(HALF):
        for p in range(P):
            s, n = divmod(P * k + p, NF)
            wbd[p, AT[k] + s - span(k)[0], :] = wsi[:, n]
    out["wbd"] = wbd
    out["wsiT"] = np.ascontiguousarray(wsi.T)
    out["bs"] = a["L0_rec_bs"]
    nine = np.arange(9)[:, None]
    out["sel9"] = np.concatenate([nine // 3 == np.arange(3), nine % 3 == np.arange(3)], axis=1).astype(f32)
    out["wdT"] = np.ascontiguousarray(a["L0_rec_Wd"].T.reshape(DENSE // P, P, E).transpose(1, 0, 2))
    out["denseT"] = np.ascontiguousarray(a["r_dense_t"].T.reshape(DENSE // P, P, B).transpose(1, 0, 2))
    out["gdbd"] = np.stack([a["L0_rec_gd"], a["L0_rec_bd"]], axis=1)
    wl_in, gsi, bsi = a["L0_rec_Wl"], a["L0_rec_gsi"], a["L0_rec_bsi"]
    wl = np.zeros((P, KC, OUT), f32)
    gb = np.zeros((P, 4, KC), f32)
    sel = np.zeros((P, 2, KC, PR), f32)
    mask = np.zeros((P, KC), np.int32)
    for p in range(P):
        for k in range(KC):
            if gram_entry(p, k):
                i, c = gram_entry(p, k)
                wl[p, k, :] = wl_in[:, (i + 1) * i // 2 + c + 1]
                gb[p, :, k] = gsi[c], gsi[i], bsi[c], bsi[i]
                sel[p, 0, k, c] = sel[p, 1, k, i] = 1
                mask[p, k] = p % PR < 4 * k + p // PR
    out |= {"wl": wl, "gb": gb, "sel": sel, "mask": mask}
    out["wlx"] = np.stack([wl_in[:, (i + 1) * i // 2] for i in range(PR)], axis=0)
    out["gbsi"] = np.stack([gsi, bsi], axis=1)
    glbl = np.stack([a["L0_rec_gl"][:KEPT], a["L0_rec_bl"][:KEPT]])
    out["glbl"] = np.ascontiguousarray(glbl.reshape(2, KEPT // P, P).transpose(2, 0, 1))
    w1 = np.concatenate([a["W_top1"][:KEPT], a["W_top1"][OUT:]], axis=0)
    out["w1"] = np.ascontiguousarray(w1.reshape(-1, P, H1).transpose(1, 0, 2))
    out["b1"] = np.ascontiguousarray(a["b_top1"].reshape(-1, P).T)
    out["w2"] = np.ascontiguousarray(a["W_top2"].reshape(-1, P, H2).transpose(1, 0, 2))
    out["b2"] = np.ascontiguousarray(a["b_top2"].reshape(-1, P).T)
    out["w3"] = np.ascontiguousarray(a["W_top3"].reshape(-1, P).T)
    return out


def kernel(**inputs):
    import concourse.bacc as bacc
    from concourse.bass_utils import run_bass_kernel_spmd

    nc = bacc.Bacc("TRN2", target_bir_lowering=False, num_devices=1)
    arrays = {f"{k}_dram": v for k, v in layouts(inputs).items()}
    t = {k[:-5]: nc.dram_tensor(k, v.shape, mybir.dt.from_np(v.dtype), kind="ExternalInput").ap()
         for k, v in arrays.items()}
    t["out"] = nc.dram_tensor("y_dram", (B, 1), F32, kind="ExternalOutput").ap()
    dlrm_tower(nc, t)
    r = run_bass_kernel_spmd(nc, [arrays], core_ids=[0])
    return r.results[0]["y_dram"]
```

```python
from contextlib import ExitStack

import numpy as np
import concourse.bass as bass
from concourse import mybir

ALU = mybir.AluOpType
ACT = mybir.ActivationFunctionType
AX_X = mybir.AxisListType.X
F32 = mybir.dt.float32
BF16 = mybir.dt.bfloat16
I32 = mybir.dt.int32

P = 128
EPS = 1e-5
B = 512
NF = 26
D = 64
E = 128
PR = 32
DENSE = 256
OUT = 512
KEPT = 384
H1 = 512
H2 = 256

GROUP = 128
NG = B // GROUP
TILES = GROUP * NF // P
PAIRS = TILES // 2
HALF = TILES // 2
QS = 16
QUARTERS = GROUP // QS
ITEMS = PR + 2
SLOTS = QS // 2
NZ = GROUP // 2
KC = PR // 8
ROW_ONE, ROW_S, ROW_XS = 32, 64, 96
ROWS_X = ROW_XS + 1


def span(tile):
    k = tile % HALF
    return P * k // NF, (P * k + P - 1) // NF


SPANS = [span(k)[1] - span(k)[0] + 1 for k in range(HALF)]
AT = [sum(SPANS[:k]) for k in range(HALF)]
NSPAN = sum(SPANS)


def pieces(tile):
    lo, hi = span(tile)
    base = (tile // HALF) * (HALF * P // NF)
    out = []
    for q in range(QUARTERS):
        a, b = max(base + lo, QS * q), min(base + hi, QS * q + QS - 1)
        if a <= b:
            out.append((q, (a - QS * q) * PR, (b - a + 1) * PR, (AT[tile % HALF] + a - base - lo) * PR))
    return out


LAST_PAIR = [((QS * NF * (q + 1) - 1) // P) // 2 for q in range(QUARTERS)]
FIRST_TILE = [QS * NF * q // P for q in range(QUARTERS)]
STEPS = NG * PAIRS
T_AHEAD, U_AHEAD = 3, 2
T_FIRST = 9
NORM_LAG, GRAM_LAG, COPY_LAG = 1, 2, 3


def due(step, lag):
    g, j = divmod(step - lag, PAIRS)
    return [(g, q) for q in range(QUARTERS) if LAST_PAIR[q] == j and 0 <= g < NG]


def gram_entry(p, k):
    i, c = p % PR, 4 * k + p // PR
    return None if i == c else (i, c) if i > c else (PR - 1 - i, PR - 1 - c)


STACKING = 16 * 2 * 2 * 4
ACT_PARTS = [(1, 2), (1, 3)]
DVE_PARTS = [(h, r) for h in range(2) for r in range(4) if (h, r) not in ACT_PARTS]
EARLY = NZ // 2

NTU, NPY = 3, 3


def wait_if_any(eng, semaphore, value):
    if value > 0:
        eng.wait_ge(semaphore, value)


def dlrm_tower(nc, t):
    ctx = ExitStack()
    with ctx:
        def sb(name, shape, dt=F32):
            return ctx.enter_context(nc.sbuf_tensor(name, shape, dt))

        def pb(name, shape):
            return ctx.enter_context(nc.psum_tensor(name, shape, F32))

        def sem(name):
            return ctx.enter_context(nc.semaphore(name))

        index_parts = sb("index_parts", [P, NG * TILES + HALF], I32)
        ids, bases = index_parts[:, 0:NG * TILES], index_parts[:, NG * TILES:]
        rows_at = sb("rows_at", [P, NG * TILES // HALF, HALF], I32)
        emb = sb("emb", [P, NG * TILES, D])
        embT = sb("embT", [P, PAIRS, P])
        proj = sb("proj", [P, PAIRS, 2, E])
        junk = sb("junk", [P, 2, E])
        u_ms = sb("u_ms", [P, PAIRS, 2])
        u_sd = sb("u_sd", [P, PAIRS, 2])
        u_r = sb("u_r", [P, PAIRS, 2])
        ysq = sb("ysq", [P, 2, QS, PR])
        y_ms = sb("y_ms", [P, QUARTERS, QS])
        y_sd = sb("y_sd", [P, QUARTERS, QS])
        y_r = sb("y_r", [P, QUARTERS, QS])
        T = sb("T", [P, GROUP, ITEMS])
        gram = sb("gram", [2 * PR, 2, ITEMS, NZ])
        zn = [sb(f"zn{i}", [P, KC, 2, NZ]) for i in range(2)]
        zr = [sb(f"zr{i}", [P, KC, 2, NZ]) for i in range(2)]
        zx = [sb(f"zx{i}", [P, 2, NZ]) for i in range(2)]
        f_bn = sb("f_bn", [P, 6])
        f_mv = sb("f_mv", [P, 2])
        f_sd = sb("f_sd", [P, 1])
        f_r = sb("f_r", [P, 1])
        znorm = sb("znorm", [P, KEPT])
        zT = sb("zT", [P, KEPT // P, GROUP])
        h1 = sb("h1", [P, H1 // P, GROUP])
        h2 = sb("h2", [P, H2 // P, GROUP])
        y_row = sb("y_row", [1, B])
        wbd = sb("wbd", [P, NSPAN, PR])
        proj_w = sb("proj_w", [P, P + 2 * E])
        ident = proj_w[:, 0:P]
        wsT = proj_w[:, P:].rearrange("p (t e) -> p t e", t=2)
        comb_w = sb("comb_w", [P, HALF * PR + NSPAN + E + 2])
        wsi_rows = comb_w[:, 0:HALF * PR].rearrange("p (k c) -> p k c", c=PR)
        in_span = comb_w[:, HALF * PR:HALF * PR + NSPAN]
        gs_b = comb_w[:, HALF * PR + NSPAN:HALF * PR + NSPAN + E]
        gdbd = comb_w[:, HALF * PR + NSPAN + E:]
        wsi_m = sb("wsi_m", [P, HALF])
        ws_m = sb("ws_m", [P, 2])
        bias9 = sb("bias9", [9, E + PR])
        sel9 = sb("sel9", [9, 3, E + PR])
        part = sb("part", [9, 3, E + PR], BF16)
        rest = sb("rest", [9, 2, E + PR])
        chosen = sb("chosen", [9, 3, E + PR])
        acc9 = sb("acc9", [9, E + PR])
        bias_l = sb("bias_l", [9, E], BF16)
        bias_r = sb("bias_r", [9, QS, PR], BF16)
        wdT = sb("wdT", [P, DENSE // P, E])
        wd_m = sb("wd_m", [P, DENSE // P])
        denseT = sb("denseT", [P, DENSE // P, B])
        xsq = sb("xsq", [P, NG, E])
        x_ms = sb("x_ms", [P, NG])
        x_sd = sb("x_sd", [P, NG])
        x_r = sb("x_r", [P, NG])
        x_rows = sb("x_rows", [P, NG, E])
        xT = sb("xT", [P, B])
        xs = sb("xs", [P, NG, 2, NZ])
        wl = sb("wl", [P, KC, OUT])
        wlx = sb("wlx", [PR, OUT])
        wl5 = sb("wl5", [P, OUT])
        gb = sb("gb", [P, 4, KC])
        gg = sb("gg", [P, 4, KC])
        sel = sb("sel", [P, 2, KC, PR])
        fold = sb("fold", [P, KC, ROWS_X])
        fold_b = sb("fold_b", [P, KC, PR])
        foldx = sb("foldx", [PR, ROWS_X])
        gbsi = sb("gbsi", [PR, 2])
        mask = sb("mask", [P, KC], I32)
        glbl = sb("glbl", [P, 2, KEPT // P])
        w1 = sb("w1", [P, (KEPT + DENSE) // P, H1])
        b1 = sb("b1", [P, H1 // P])
        w2 = sb("w2", [P, H1 // P, H2])
        b2 = sb("b2", [P, H2 // P])
        w3 = sb("w3", [P, H2 // P])
        ones = sb("ones", [P, 9])
        eps = sb("eps", [P, 1])
        warm = sb("warm", [P, 1])

        TU = [pb(f"tu{i}", [P, 512]) for i in range(NTU)]
        PY = [pb(f"py{i}", [P, QS, PR]) for i in range(NPY)]
        PZ = pb("pz", [P, 512])
        PZv = PZ[:, 0:SLOTS * ITEMS].rearrange("p (b c) -> p b c", c=ITEMS)
        PF = pb("pf", [P, 512])

        l_ids = sem("l_ids")
        l_proj = sem("l_proj")
        l_comb = sem("l_comb")
        l_nine = sem("l_nine")
        l_dense = sem("l_dense")
        l_late = sem("l_late")
        rows_ready = sem("rows_ready")
        gathered = [sem(f"gathered{pair}") for pair in range(STEPS)]
        consts_ready = sem("consts_ready")
        t_done = sem("t_done")
        u_done = sem("u_done")
        y_done = sem("y_done")
        z_done = sem("z_done")
        f_done = sem("f_done")
        tz_done = sem("tz_done")
        m1_done = sem("m1_done")
        m2_done = sem("m2_done")
        m3_done = sem("m3_done")
        x_done = sem("x_done")
        sc_done = sem("sc_done")
        sc_ready = sem("sc_ready")
        xs_done = sem("xs_done")
        xt_done = sem("xt_done")
        w5_done = sem("w5_done")
        embT_ready = sem("embT_ready")
        u_ms_ready = sem("u_ms_ready")
        u_sd_ready = sem("u_sd_ready")
        ysq_ready = sem("ysq_ready")
        y_sd_ready = sem("y_sd_ready")
        xcol_ready = sem("xcol_ready")
        gram_ready = sem("gram_ready")
        f_sd_ready = sem("f_sd_ready")
        zT_ready = sem("zT_ready")
        h1_ready = sem("h1_ready")
        h2_ready = sem("h2_ready")
        y_ready = sem("y_ready")
        x_ms_ready = sem("x_ms_ready")
        xT_ready = sem("xT_ready")
        x_sd_ready = sem("x_sd_ready")
        xs_ready = sem("xs_ready")
        zx_xs_ready = sem("zx_xs_ready")
        wl5_ready = sem("wl5_ready")
        dve_setup = sem("dve_setup")
        wsT_ready = sem("wsT_ready")
        wbd_ready = sem("wbd_ready")
        wsi_ready = sem("wsi_ready")
        wd_ready = sem("wd_ready")
        bias_ready = sem("bias_ready")
        x_r_ready = sem("x_r_ready")
        x_rows_ready = sem("x_rows_ready")
        wl_ready = sem("wl_ready")
        fold_ready = sem("fold_ready")
        u_r_ready = sem("u_r_ready")
        proj_ready = sem("proj_ready")
        y_ms_ready = sem("y_ms_ready")
        y_r_ready = sem("y_r_ready")
        T_ready = sem("T_ready")
        f_bn_ready = sem("f_bn_ready")
        f_mv_ready = sem("f_mv_ready")
        f_r_ready = sem("f_r_ready")
        znorm_ready = sem("znorm_ready")
        stacked = [sem(f"stacked{i}") for i in range(2)]
        late_stacked = sem("late_stacked")
        linear_ready = sem("linear_ready")
        turned = sem("turned")
        merged = sem("merged")
        stored = sem("stored")

        def f_bank(g):
            return PF if g < NG - 1 else PY[0][:, :, :].rearrange("p b c -> p (b c)")

        def layer1(g, m):
            return PF[:, P * m:P * m + P] if g < NG - 1 else [*TU, PY[2][:, :, :].rearrange("p b c -> p (b c)")][m][:, 0:P]

        def layer2(g, m):
            return PF[:, P * m:P * m + P] if g < NG - 1 else [PF, PZ][m][:, 0:P]

        def layer3(g):
            return PF[0:1, 0:GROUP] if g < NG - 1 else TU[0][0:1, 0:GROUP]

        block = ctx.enter_context(nc.Block())

        @block.sync
        def _(sp):
            sp.dma_start(index_parts[:, :], t["index_parts"]).then_inc(l_ids, 16)
            sp.dma_start(proj_w[:, :], t["proj_w"]).then_inc(l_proj, 16)
            sp.dma_start(bias9[:, 0:E], t["bs"].partition_broadcast(9)).then_inc(l_nine, 16)
            sp.dma_start(sel9[:, :, :], t["sel9"]).then_inc(l_nine, 16)
            sp.wait_ge(gathered[0], 32)
            for dst, src in ((wl, "wl"), (wlx, "wlx"), (gb, "gb"), (sel, "sel"), (gbsi, "gbsi"), (mask, "mask"),
                             (glbl, "glbl"), (w1, "w1"), (b1, "b1"), (w2, "w2"), (b2, "b2"), (w3, "w3")):
                sp.dma_start(dst[tuple(slice(None) for _ in dst.shape)], t[src]).then_inc(l_late, 16)

            def stack(g, samples):
                sp.wait_ge(gram_ready, g * QUARTERS + samples.stop // SLOTS)
                wait_if_any(sp, f_done, g - 1)
                for h in range(2):
                    of = gram[PR * h:PR * h + PR, g % 2, :, samples]
                    for r in range(4):
                        sp.dma_start(zn[g % 2][PR * r:PR * r + PR, :, h, samples], of[:, r:PR // 2:4, :]).then_inc(stacked[g % 2], 16)
                        sp.dma_start(zr[g % 2][PR * r:PR * r + PR, :, h, samples],
                                     of[:, PR - 1 - r:PR // 2 - 1:-4, :]).then_inc(stacked[g % 2], 16)

            sp.wait_ge(consts_ready, 9)
            for g in range(NG - 1):
                stack(g, slice(0, NZ))
            stack(NG - 1, slice(0, EARLY))

            sp.wait_ge(y_ready, NG)
            sp.dma_start(t["out"].rearrange("b one -> one b"), y_row[:, :]).then_inc(stored, 16)
            sp.wait_ge(stored, 16)

        @block.gpsimd
        def _(pool):
            pool.memset(eps[:, :], EPS).then_inc(consts_ready, 1)
            pool.memset(ones[:, :], 1.0).then_inc(consts_ready, 1)
            pool.wait_ge(l_ids, 16)

            def gather(tiles):
                for k in tiles:
                    pool.indirect_dma_start(
                        emb[:, k, :], None, t["tables"],
                        bass.IndirectOffsetOnAxis(ap=rows_at[:, k // HALF, k % HALF:k % HALF + 1], axis=0),
                    ).then_inc(gathered[k // 2], 16)

            pool.tensor_tensor(rows_at[:, :, :], ids.rearrange("p (h k) -> p h k", k=HALF),
                               bases.unsqueeze(1).to_broadcast([P, NG * TILES // HALF, HALF]),
                               ALU.add).then_inc(rows_ready, 1)
            pool.wait_ge(rows_ready, 1)
            gather(range(HALF))
            pool.memset(T[:, :, PR + 1:PR + 2], 1.0).then_inc(consts_ready, 1)
            pool.memset(fold[:, :, :], 0.0).then_inc(consts_ready, 1)
            pool.memset(foldx[:, :], 0.0).then_inc(consts_ready, 1)
            for i in range(2):
                pool.memset(zx[i][:, :, :], 0.0).then_inc(consts_ready, 1)
            pool.wait_ge(consts_ready, 7)
            for i in range(2):
                pool.memset(zx[i][ROW_ONE:ROW_ONE + 1, :, :], 1.0).then_inc(consts_ready, 1)
            pool.wait_ge(consts_ready, 9)
            gather(range(HALF, NG * TILES))

        @block.tensor
        def _(pe):
            def transposes(g, j):
                pe.wait_ge(gathered[g * PAIRS + j], 32)
                wait_if_any(pe, proj_ready, g * PAIRS + j + 1 - NTU)
                pe.transpose(TU[(PAIRS * g + j) % NTU][:, 0:P], emb[:, g * TILES + 2 * j:g * TILES + 2 * j + 2, :].rearrange("p t d -> p (t d)"),
                             ident).then_inc(t_done, 1)

            def project(g, j):
                pe.wait_ge(embT_ready, g * PAIRS + j + 1)
                pe.matmul(TU[(PAIRS * g + j) % NTU][:, P:P + 2 * E], embT[:, j, :], proj_w[:, P:],
                          start=True, stop=True).then_inc(u_done, 1)

            def combine(g, j):
                pe.wait_ge(proj_ready, g * PAIRS + j + 1)
                for tile in (2 * j, 2 * j + 1):
                    if g == 0 and tile < HALF:
                        pe.wait_ge(wbd_ready, tile + 1)
                    for q, col, n, at in pieces(tile):
                        if tile == FIRST_TILE[q]:
                            wait_if_any(pe, T_ready, g * QUARTERS + q + 1 - NPY)
                            pe.matmul(PY[(QUARTERS * g + q) % NPY][:, :, :].rearrange("p b c -> p (b c)"), bias_l[:, :],
                                      bias_r[:, :, :].rearrange("p b c -> p (b c)"),
                                      start=True, stop=False, skip_group_check=True)
                        mm = pe.matmul(PY[(QUARTERS * g + q) % NPY][:, :, :].rearrange("p b c -> p (b c)")[:, col:col + n],
                                       proj[:, j, tile % 2, :],
                                       wbd[:, :, :].rearrange("p b c -> p (b c)")[:, at:at + n],
                                       start=False, stop=col + n == QS * PR, skip_group_check=True)
                mm.then_inc(y_done, 1)

            def gram_products(g, q):
                pe.wait_ge(T_ready, g * QUARTERS + q + 1)
                if q == 0:
                    pe.wait_ge(xcol_ready, g + 1)
                wait_if_any(pe, gram_ready, g * QUARTERS + q)
                for s in range(QS):
                    h, b = s % 2, s // 2
                    of = T[:, QS * q + s, 0:ITEMS]
                    mm = pe.matmul(PZ[PR * h:PR * h + PR, ITEMS * b:ITEMS * (b + 1)], of[:, 0:PR], of,
                                   start=True, stop=True)
                mm.then_inc(z_done, 1)

            def flat_layer(g, chunks):
                for k in chunks:
                    if k == 0:
                        pe.wait_ge(merged, g + 1)
                        pe.wait_ge(zx_xs_ready, g + 1)
                        if g < NG - 1:
                            wait_if_any(pe, y_ready, g)
                        if g == 0:
                            pe.wait_ge(wl5_ready, 1)
                            pe.wait_ge(wl_ready, KC)
                    if k < KC:
                        mm = pe.matmul(f_bank(g)[:, :], zn[g % 2][:, k, :, :].rearrange("p h b -> p (h b)"), wl[:, k, :],
                                       start=(k == 0), stop=False)
                    else:
                        pe.wait_ge(linear_ready, g + 1)
                        pe.matmul(f_bank(g)[:, :], zx[g % 2][0:ROWS_X, :, :].rearrange("p h b -> p (h b)"), wl5[0:ROWS_X, :],
                                  start=False, stop=True).then_inc(f_done, 1)

            def z_transposes(g):
                pe.wait_ge(znorm_ready, g + 1)
                for c in range(KEPT // P):
                    mm = pe.transpose(f_bank(g)[:, P * c:P * c + P], znorm[:, P * c:P * c + P], ident)
                mm.then_inc(tz_done, 1)

            def mlp1(g, columns, chunks=(3, 4, 0, 1, 2)):
                if 0 in chunks:
                    pe.wait_ge(zT_ready, g + 1)
                for m in columns:
                    for c in chunks:
                        rhs = zT[:, c, :] if c < 3 else denseT[:, c - 3, GROUP * g:GROUP * (g + 1)]
                        mm = pe.matmul(layer1(g, m), w1[:, c, P * m:P * m + P], rhs,
                                       start=(c == 3), stop=(c == 2))
                    if chunks[-1] == 2:
                        mm.then_inc(m1_done, 1)

            def mlp2(g):
                if g < NG - 1:
                    pe.wait_ge(h1_ready, (g + 1) * (H1 // P))
                    for m in range(H2 // P):
                        for c in range(H1 // P):
                            mm = pe.matmul(layer2(g, m), w2[:, c, P * m:P * m + P], h1[:, c, :],
                                           start=(c == 0), stop=(c == H1 // P - 1))
                else:
                    pe.wait_ge(y_ready, g)
                    for c in range(H1 // P):
                        pe.wait_ge(h1_ready, g * (H1 // P) + c + 1)
                        for m in range(H2 // P):
                            mm = pe.matmul(layer2(g, m), w2[:, c, P * m:P * m + P], h1[:, c, :],
                                           start=(c == 0), stop=(c == H1 // P - 1))
                mm.then_inc(m2_done, 1)

            def mlp3(g):
                pe.wait_ge(h2_ready, g + 1)
                for c in range(H2 // P):
                    mm = pe.matmul(layer3(g), w3[:, c:c + 1], h2[:, c, :],
                                   start=(c == 0), stop=(c == H2 // P - 1))
                mm.then_inc(m3_done, 1)

            def last_layers(g, since):
                if since == 9:
                    flat_layer(g, (0, 1))
                if since == 10:
                    flat_layer(g, (2, 3))
                if since == 11:
                    flat_layer(g, (4,))
                if since == 14:
                    z_transposes(g)
                if since == 15:
                    mlp1(g, (0, 1))
                if since == 16:
                    mlp1(g, (2, 3))
                if since == 18:
                    mlp2(g)
                if since == 20:
                    mlp3(g)

            def bias_sums():
                pe.wait_ge(wsi_ready, 1)
                pe.matmul(PZ[0:9, 0:PR], ones[0:NF, :], wsi_rows[0:NF, 0, :], start=True, stop=True).then_inc(sc_done, 1)

            def x_projected():
                pe.wait_ge(wd_ready, 1)
                pe.wait_ge(l_dense, 32)
                for g in range(NG):
                    for c in range(DENSE // P):
                        mm = pe.matmul(PF[:, E * g:E * g + E], denseT[:, c, GROUP * g:GROUP * (g + 1)], wdT[:, c, :],
                                       start=(c == 0), stop=(c == DENSE // P - 1))
                mm.then_inc(x_done, 1)

            def x_transposes():
                pe.wait_ge(x_rows_ready, 1)
                for g in range(NG):
                    mm = pe.transpose(PF[:, GROUP * g:GROUP * (g + 1)], x_rows[:, g, :], ident)
                mm.then_inc(xt_done, 1)

            def x_sums():
                pe.wait_ge(xT_ready, 1)
                pe.matmul(PF[0:1, :], ones[:, 0:1], xT[:, :], start=True, stop=True).then_inc(xs_done, 1)

            def folded_weights():
                pe.wait_ge(fold_ready, 1)
                pe.wait_ge(xs_ready, 1)
                for k in range(KC):
                    pe.matmul(PF[0:ROWS_X, :], fold[:, k, :], wl[:, k, :], start=(k == 0), stop=False)
                pe.matmul(PF[0:ROWS_X, :], foldx[:, :], wlx[:, :], start=False, stop=True).then_inc(w5_done, 1)

            pe.wait_ge(consts_ready, 2)
            pe.wait_ge(l_proj, 16)
            bias_sums()
            transposes(0, 0)
            pe.wait_ge(wsT_ready, 1)
            project(0, 0)
            x_projected()
            transposes(0, 1)
            project(0, 1)
            pe.wait_ge(bias_ready, 1)
            for pair in range(2, T_AHEAD):
                transposes(0, pair)
            for step in range(STEPS):
                g, j = divmod(step, PAIRS)
                if T_FIRST <= step < STEPS - T_AHEAD:
                    transposes(*divmod(step + T_AHEAD, PAIRS))
                combine(g, j)
                if step + U_AHEAD < STEPS:
                    project(*divmod(step + U_AHEAD, PAIRS))
                if step < T_FIRST:
                    transposes(*divmod(step + T_AHEAD, PAIRS))
                if step == 0:
                    x_transposes()
                if step == 3:
                    x_sums()
                if step == 8:
                    folded_weights()
                for group, quarter in due(step, GRAM_LAG):
                    gram_products(group, quarter)
                for group in range(g):
                    last_layers(group, step - PAIRS * (group + 1))
            last = NG - 1
            gram_products(last, QUARTERS - 2)
            mlp1(last, (0, 1, 2, 3), (3, 4))
            z_transposes(last - 1)
            gram_products(last, QUARTERS - 1)
            mlp1(last - 1, (0, 1, 2, 3))
            flat_layer(last, (0, 1, 2, 3, 4))
            mlp2(last - 1)
            mlp3(last - 1)
            z_transposes(last)
            mlp1(last, (0, 1, 2, 3), (0, 1, 2))
            mlp2(last)
            mlp3(last)

        @block.scalar
        def _(act):
            act.dma_start(comb_w[:, :], t["comb_w"]).then_inc(l_comb, 16)
            act.dma_start(wdT[:, :, :], t["wdT"]).then_inc(l_dense, 16)
            act.dma_start(denseT[:, :, :], t["denseT"]).then_inc(l_dense, 16)

            def embT_copy(g, j):
                act.wait_ge(t_done, g * PAIRS + j + 1)
                act.activation(embT[:, j, :], TU[(PAIRS * g + j) % NTU][:, 0:P], ACT.Copy).then_inc(embT_ready, 1)

            def u_spread(g, j):
                act.wait_ge(u_done, g * PAIRS + j + 1)
                for i in range(2):
                    a = act.activation(junk[:, i, :], TU[(PAIRS * g + j) % NTU][:, P + E * i:P + E * (i + 1)], ACT.Square,
                                       scale=float(E) ** -0.5, accum_out=u_ms[:, j, i:i + 1])
                a.then_inc(u_ms_ready, 1)
                act.wait_ge(u_ms_ready, g * PAIRS + j + 1)
                act.activation(u_sd[:, j, :], u_ms[:, j, :], ACT.Sqrt, bias=eps[:, :]).then_inc(u_sd_ready, 1)

            def y_square(g, q):
                act.wait_ge(y_done, g * PAIRS + LAST_PAIR[q] + 1)
                act.activation(ysq[:, q % 2, :, :], PY[(QUARTERS * g + q) % NPY][:, :, :], ACT.Square,
                               scale=float(PR) ** -0.5).then_inc(ysq_ready, 1)

            def y_spread(g, q):
                act.wait_ge(y_ms_ready, g * QUARTERS + q + 1)
                act.activation(y_sd[:, q, :], y_ms[:, q, :], ACT.Sqrt, bias=eps[:, :]).then_inc(y_sd_ready, 1)

            def gram_copy(g, q):
                act.wait_ge(z_done, g * QUARTERS + q + 1)
                wait_if_any(act, stacked[g % 2], STACKING * (g // 2))
                act.activation(gram[:, g % 2, :, SLOTS * q:SLOTS * (q + 1)], PZv[0:2 * PR].rearrange("p b c -> p c b"),
                               ACT.Copy).then_inc(gram_ready, 1)

            def x_columns(g):
                wait_if_any(act, z_done, g * QUARTERS)
                act.activation(T[:, :, PR], xT[:, bass.ds(g * GROUP, GROUP)], ACT.Copy).then_inc(xcol_ready, 1)

            def x_sums_copy(g):
                wait_if_any(act, f_done, g - 1)
                act.activation(zx[g % 2][ROW_XS:ROW_XS + 1, :, :].rearrange("p h b -> p (h b)"),
                               xs[ROW_XS:ROW_XS + 1, g, :, :].rearrange("p h b -> p (h b)"),
                               ACT.Copy).then_inc(zx_xs_ready, 1)

            def f_spread(g):
                act.wait_ge(f_mv_ready, g + 1)
                act.activation(f_sd[:, :], f_mv[:, 1:2], ACT.Sqrt, bias=eps[:, :]).then_inc(f_sd_ready, 1)

            def z_scaled(g):
                act.wait_ge(tz_done, g + 1)
                for c in range(KEPT // P):
                    a = act.activation(zT[:, c, :].rearrange("p (b h) -> p h b", h=2),
                                       f_bank(g)[:, P * c:P * c + P].rearrange("p (h b) -> p h b", h=2),
                                       ACT.Identity, scale=glbl[:, 0, c:c + 1], bias=glbl[:, 1, c:c + 1])
                a.then_inc(zT_ready, 1)

            def h1_relu(g):
                if g < NG - 1:
                    act.wait_ge(m1_done, (g + 1) * (H1 // P))
                for m in range(H1 // P):
                    if g == NG - 1:
                        act.wait_ge(m1_done, g * (H1 // P) + m + 1)
                    act.activation(h1[:, m, :], layer1(g, m), ACT.Relu, bias=b1[:, m:m + 1]).then_inc(h1_ready, 1)

            def h2_relu(g):
                act.wait_ge(m2_done, g + 1)
                for m in range(H2 // P):
                    a = act.activation(h2[:, m, :], layer2(g, m), ACT.Relu, bias=b2[:, m:m + 1])
                a.then_inc(h2_ready, 1)

            def y_copy(g):
                act.wait_ge(m3_done, g + 1)
                act.activation(y_row[0:1, GROUP * g:GROUP * (g + 1)], layer3(g),
                               ACT.Copy).then_inc(y_ready, 1)

            def last_layers(g, since):
                if since == 3:
                    x_sums_copy(g)
                if since == 12:
                    f_spread(g)
                if since == 14:
                    z_scaled(g)
                if since == 16:
                    h1_relu(g)
                if since == 19:
                    h2_relu(g)
                if since == 21:
                    y_copy(g)

            def late_stack(g, samples):
                for h, r in ACT_PARTS:
                    of = gram[PR * h:PR * h + PR, g % 2, :, samples]
                    act.activation(zn[g % 2][PR * r:PR * r + PR, :, h, samples], of[:, r:PR // 2:4, :], ACT.Copy)
                    a = act.activation(zr[g % 2][PR * r:PR * r + PR, :, h, samples], of[:, PR - 1 - r:PR // 2 - 1:-4, :], ACT.Copy)
                a.then_inc(late_stacked, 1)

            def x_spread():
                act.wait_ge(x_done, 1)
                for g in range(NG):
                    a = act.activation(xsq[:, g, :], PF[:, E * g:E * g + E], ACT.Square, scale=float(E) ** -0.5,
                                       accum_out=x_ms[:, g:g + 1])
                a.then_inc(x_ms_ready, 1)
                act.wait_ge(x_ms_ready, 1)
                act.activation(x_sd[:, :], x_ms[:, :], ACT.Sqrt, bias=eps[:, :]).then_inc(x_sd_ready, 1)

            def x_scaled():
                act.wait_ge(xt_done, 1)
                act.activation(xT[:, :], PF[:, :], ACT.Identity, scale=gdbd[:, 0:1],
                               bias=gdbd[:, 1:2]).then_inc(xT_ready, 1)

            act.wait_ge(consts_ready, 2)
            act.activation(warm[:, :], eps[:, :], ACT.Sqrt)
            act.wait_ge(l_comb, 16)
            embT_copy(0, 0)
            u_spread(0, 0)
            embT_copy(0, 1)
            x_spread()
            u_spread(0, 1)
            for pair in range(2, T_AHEAD):
                embT_copy(0, pair)
            for step in range(STEPS):
                g, j = divmod(step, PAIRS)
                if step == 12:
                    act.wait_ge(l_late, 16 * 12)
                    act.wait_ge(consts_ready, 9)
                if T_FIRST <= step < STEPS - T_AHEAD:
                    embT_copy(*divmod(step + T_AHEAD, PAIRS))
                for group, quarter in due(step, COPY_LAG):
                    gram_copy(group, quarter)
                for group, quarter in due(step, 0):
                    y_square(group, quarter)
                if step + U_AHEAD < STEPS:
                    u_spread(*divmod(step + U_AHEAD, PAIRS))
                if step < T_FIRST:
                    embT_copy(*divmod(step + T_AHEAD, PAIRS))
                for group, quarter in due(step, 0):
                    y_spread(group, quarter)
                if step == 1:
                    x_scaled()
                if j == 2 and step < STEPS:
                    x_columns(g)
                if step == 4:
                    act.wait_ge(xs_done, 1)
                    act.activation(xs[ROW_XS:ROW_XS + 1, :, :, :].rearrange("p g h b -> p g b h"),
                                   PF[0:1, :].rearrange("p (g b h) -> p g b h", g=NG, h=2),
                                   ACT.Copy).then_inc(xs_ready, 1)
                if step == 10:
                    act.wait_ge(w5_done, 1)
                    act.activation(wl5[0:ROWS_X, :], PF[0:ROWS_X, :], ACT.Copy).then_inc(wl5_ready, 1)
                for group in range(g):
                    last_layers(group, step - PAIRS * (group + 1))
            last = NG - 1
            gram_copy(last, QUARTERS - 2)
            z_scaled(last - 1)
            gram_copy(last, QUARTERS - 1)
            act.wait_ge(gram_ready, NG * QUARTERS)
            late_stack(last, slice(EARLY, NZ))
            x_sums_copy(last)
            h1_relu(last - 1)
            f_spread(last)
            h2_relu(last - 1)
            z_scaled(last)
            y_copy(last - 1)
            h1_relu(last)
            h2_relu(last)
            y_copy(last)

        @block.vector
        def _(dve):
            steps = [0]

            def chain(ins):
                steps[0] += 1
                ins.then_inc(dve_setup, 1)
                dve.wait_ge(dve_setup, steps[0])

            def centre(w, m, n):
                chain(dve.tensor_reduce(m, w, AX_X, ALU.add))
                chain(dve.tensor_scalar(m, m, -1.0 / n, None, ALU.mult))
                bc = m.unsqueeze(2).to_broadcast([*w.shape]) if len(w.shape) == 3 else m.to_broadcast([*w.shape])
                return dve.tensor_tensor(w, w, bc, ALU.add)

            def bias_parts():
                dve.wait_ge(l_nine, 32)
                dve.wait_ge(sc_done, 1)
                chain(dve.tensor_copy(bias9[:, E:], PZ[0:9, 0:PR]))
                chain(dve.tensor_copy(part[:, 0, :], bias9[:, :]))
                chain(dve.tensor_tensor(rest[:, 0, :], bias9[:, :], part[:, 0, :], ALU.subtract))
                chain(dve.tensor_copy(part[:, 1, :], rest[:, 0, :]))
                chain(dve.tensor_tensor(rest[:, 1, :], rest[:, 0, :], part[:, 1, :], ALU.subtract))
                chain(dve.tensor_copy(part[:, 2, :], rest[:, 1, :]))
                chain(dve.tensor_tensor(chosen[:, :, :], part[:, :, :], sel9[:, :, :], ALU.mult))
                chain(dve.tensor_reduce(acc9[:, :], chosen[:, :, :].rearrange("p i w -> p w i"), AX_X, ALU.add))
                chain(dve.tensor_copy(bias_l[:, :], acc9[:, 0:E]))
                dve.tensor_copy(bias_r[:, :, :], acc9[:, E:].unsqueeze(1).to_broadcast([9, QS, PR])).then_inc(bias_ready, 1)

            def place(k):
                n = SPANS[k]
                dve.tensor_tensor(wbd[:, AT[k]:AT[k] + n, :], wsi_rows[:, k, :].unsqueeze(1).to_broadcast([P, n, PR]),
                                  in_span[:, AT[k]:AT[k] + n].unsqueeze(2).to_broadcast([P, n, PR]),
                                  ALU.mult).then_inc(wbd_ready, 1)

            def x_normalised():
                dve.wait_ge(x_sd_ready, 1)
                dve.reciprocal(x_r[:, :], x_sd[:, :]).then_inc(x_r_ready, 1)
                dve.wait_ge(x_r_ready, 1)
                dve.tensor_tensor(x_rows[:, :, :], PF[:, :].rearrange("p (g e) -> p g e", e=E),
                                  x_r[:, :].unsqueeze(2).to_broadcast([P, NG, E]), ALU.mult).then_inc(x_rows_ready, 1)

            def fold_weights():
                dve.wait_ge(l_late, 16 * 12)
                dve.wait_ge(consts_ready, 9)
                ga, gB, ba, bB = (gb[:, i, :] for i in range(4))
                chain(dve.tensor_tensor(gg[:, 0, :], ga, gB, ALU.mult))
                chain(dve.tensor_tensor(gg[:, 1, :], ga, bB, ALU.mult))
                chain(dve.tensor_tensor(gg[:, 2, :], gB, ba, ALU.mult))
                chain(dve.tensor_tensor(gg[:, 3, :], ba, bB, ALU.mult))
                chain(dve.tensor_tensor(fold_b[:, :, :], sel[:, 1, :, :],
                                        gg[:, 2, :].unsqueeze(2).to_broadcast([P, KC, PR]), ALU.mult))
                to = fold[:, :, ROW_S:ROW_S + PR]
                chain(dve.tensor_tensor(to, sel[:, 0, :, :], gg[:, 1, :].unsqueeze(2).to_broadcast([P, KC, PR]), ALU.mult))
                chain(dve.tensor_tensor(to, to, fold_b[:, :, :], ALU.add))
                chain(dve.tensor_scalar(fold[:, :, ROW_ONE:ROW_ONE + 1], gg[:, 3, :].unsqueeze(2), float(E), None,
                                        ALU.mult))
                chain(dve.tensor_scalar(foldx[:, 0:PR], ident[0:PR, 0:PR], gbsi[:, 0:1], None, ALU.mult))
                dve.tensor_copy(foldx[:, ROW_XS:ROW_XS + 1], gbsi[:, 1:2]).then_inc(fold_ready, 1)

            def scale_wl(k):
                dve.wait_ge(w5_done, 1)
                dve.tensor_scalar(wl[:, k, :], wl[:, k, :], gg[:, 0, k:k + 1], None, ALU.mult).then_inc(wl_ready, 1)

            def project(g, j):
                dve.wait_ge(u_sd_ready, g * PAIRS + j + 1)
                dve.reciprocal(u_r[:, j, :], u_sd[:, j, :]).then_inc(u_r_ready, 1)
                dve.wait_ge(u_r_ready, g * PAIRS + j + 1)
                for i in range(2):
                    a = dve.scalar_tensor_tensor(out=proj[:, j, i, :], in0=TU[(PAIRS * g + j) % NTU][:, P + E * i:P + E * (i + 1)],
                                                 scalar=u_r[:, j, i:i + 1], in1=gs_b,
                                                 op0=ALU.mult, op1=ALU.mult)
                a.then_inc(proj_ready, 1)

            def y_sums(g, q):
                dve.wait_ge(ysq_ready, g * QUARTERS + q + 1)
                dve.tensor_reduce(y_ms[:, q, :], ysq[:, q % 2, :, :], AX_X, ALU.add).then_inc(y_ms_ready, 1)

            def normalise(g, q):
                dve.wait_ge(y_sd_ready, g * QUARTERS + q + 1)
                dve.reciprocal(y_r[:, q, :], y_sd[:, q, :]).then_inc(y_r_ready, 1)
                dve.wait_ge(y_r_ready, g * QUARTERS + q + 1)
                dve.tensor_tensor(T[:, QS * q:QS * (q + 1), 0:PR], PY[(QUARTERS * g + q) % NPY][:, :, :],
                                  y_r[:, q, :].unsqueeze(2).to_broadcast([P, QS, PR]), ALU.mult).then_inc(T_ready, 1)

            def merge(g):
                flat = zr[g % 2][:, :, :, :].rearrange("p k h b -> p (k h b)")
                dve.stream_shuffle(flat, flat, [PR - 1 - i for i in range(PR)]).then_inc(turned, 1)
                dve.wait_ge(turned, g + 1)
                dve.copy_predicated(zn[g % 2][:, :, :, :].rearrange("p k h b -> p k (h b)"),
                                    mask[:, :].unsqueeze(2).to_broadcast([P, KC, GROUP]),
                                    zr[g % 2][:, :, :, :].rearrange("p k h b -> p k (h b)")).then_inc(merged, 1)

            def late_stack(g, samples):
                for h, r in DVE_PARTS:
                    of = gram[PR * h:PR * h + PR, g % 2, :, samples]
                    dve.tensor_copy(zn[g % 2][PR * r:PR * r + PR, :, h, samples], of[:, r:PR // 2:4, :])
                    a = dve.tensor_copy(zr[g % 2][PR * r:PR * r + PR, :, h, samples], of[:, PR - 1 - r:PR // 2 - 1:-4, :])
                a.then_inc(late_stacked, 1)

            def z_stats(g):
                dve.wait_ge(f_done, g + 1)
                dve.bn_stats(f_bn[:, :], f_bank(g)[:, :]).then_inc(f_bn_ready, 1)
                dve.wait_ge(f_bn_ready, g + 1)
                dve.bn_aggr(f_mv[:, :], f_bn[:, :]).then_inc(f_mv_ready, 1)

            def z_normalised(g):
                dve.wait_ge(f_sd_ready, g + 1)
                dve.reciprocal(f_r[:, :], f_sd[:, :]).then_inc(f_r_ready, 1)
                dve.wait_ge(f_r_ready, g + 1)
                dve.tensor_scalar(znorm[:, :], f_bank(g)[:, 0:KEPT], f_mv[:, 0:1], f_r[:, :],
                                  ALU.subtract, ALU.mult).then_inc(znorm_ready, 1)

            def linear_features(g):
                dve.wait_ge(gram_ready, (g + 1) * QUARTERS)
                wait_if_any(dve, f_done, g - 1)
                for h in range(2):
                    of = gram[PR * h:PR * h + PR, g % 2, :, :]
                    dve.tensor_copy(zx[g % 2][0:PR, h, :], of[:, PR, :])
                    a = dve.tensor_copy(zx[g % 2][ROW_S:ROW_S + PR, h, :], of[:, PR + 1, :])
                a.then_inc(linear_ready, 1)

            def last_layers(g, since):
                if since == 4:
                    linear_features(g)
                if since == 8:
                    dve.wait_ge(stacked[g % 2], STACKING * (g // 2 + 1))
                    merge(g)
                if since == 12:
                    z_stats(g)
                if since == 13:
                    z_normalised(g)

            dve.wait_ge(l_proj, 16)
            centre(wsT, ws_m[:, :], E).then_inc(wsT_ready, 1)
            dve.wait_ge(l_comb, 16)
            chain(centre(wsi_rows, wsi_m[:, :], PR))
            dve.sem_inc(wsi_ready, 1)
            place(0)
            place(1)
            dve.wait_ge(l_dense, 32)
            centre(wdT[:, :, :], wd_m[:, :], E).then_inc(wd_ready, 1)
            project(0, 0)
            bias_parts()
            place(2)
            place(3)
            project(0, 1)
            x_normalised()
            for step in range(STEPS):
                g, j = divmod(step, PAIRS)
                for tile in (2 * step + 4, 2 * step + 5):
                    if tile < HALF:
                        place(tile)
                for group, quarter in due(step, NORM_LAG):
                    normalise(group, quarter)
                for group, quarter in due(step, 0):
                    y_sums(group, quarter)
                if step + U_AHEAD < STEPS:
                    project(*divmod(step + U_AHEAD, PAIRS))
                if step == 6:
                    fold_weights()
                if 10 <= step < 10 + KC:
                    scale_wl(step - 10)
                for group in range(g):
                    last_layers(group, step - PAIRS * (group + 1))
            last = NG - 1
            z_normalised(last - 1)
            normalise(last, QUARTERS - 1)
            dve.wait_ge(stacked[last % 2], STACKING * (last // 2 + 1))
            dve.wait_ge(gram_ready, NG * QUARTERS)
            late_stack(last, slice(EARLY, NZ))
            dve.wait_ge(late_stacked, 2)
            merge(last)
            linear_features(last)
            z_stats(last)
            z_normalised(last)


def layouts(inputs):
    f32 = np.float32
    a = {k: np.asarray(v) for k, v in inputs.items()}
    tables = [a[f"tbl_{f}"] for f in range(NF)]
    base = np.cumsum([0] + [x.shape[0] for x in tables[:-1]]).astype(np.int32)
    row = np.arange(HALF * P)
    out = {"tables": np.concatenate(tables, axis=0)}
    ids = a["ids"].reshape(NG * TILES, P).T
    out["index_parts"] = np.concatenate([ids, base[row % NF].reshape(HALF, P).T], axis=1)
    wsT = np.zeros((2, D, 2, E), f32)
    wsT[0, :, 0] = wsT[1, :, 1] = a["L0_rec_Ws"].T
    out["proj_w"] = np.concatenate([np.eye(P, dtype=f32), wsT.reshape(P, 2 * E)], axis=1)
    in_span = np.zeros((P, NSPAN), f32)
    for k in range(HALF):
        for p in range(P):
            in_span[p, AT[k] + (P * k + p) // NF - span(k)[0]] = 1
    wsi_rows = a["L0_rec_Wsi"].T[(row % NF).reshape(HALF, P).T]
    out["comb_w"] = np.concatenate([wsi_rows.reshape(P, HALF * PR), in_span, np.tile(a["L0_rec_gs"], (P, 1)),
                                    a["L0_rec_gd"][:, None], a["L0_rec_bd"][:, None]], axis=1)
    out["bs"] = a["L0_rec_bs"]
    nine = np.arange(9)[:, None]
    sel9 = np.zeros((9, 3, E + PR), f32)
    sel9[:, :, :E] = (nine // 3 == np.arange(3))[:, :, None]
    sel9[:, :, E:] = (nine % 3 == np.arange(3))[:, :, None]
    out["sel9"] = sel9
    out["wdT"] = np.ascontiguousarray(a["L0_rec_Wd"].T.reshape(DENSE // P, P, E).transpose(1, 0, 2))
    out["denseT"] = np.ascontiguousarray(a["r_dense_t"].T.reshape(DENSE // P, P, B).transpose(1, 0, 2))
    wl_in, gsi, bsi = a["L0_rec_Wl"], a["L0_rec_gsi"], a["L0_rec_bsi"]
    wl = np.zeros((P, KC, OUT), f32)
    gb = np.zeros((P, 4, KC), f32)
    sel = np.zeros((P, 2, KC, PR), f32)
    mask = np.zeros((P, KC), np.int32)
    for p in range(P):
        for k in range(KC):
            if gram_entry(p, k):
                i, c = gram_entry(p, k)
                wl[p, k, :] = wl_in[:, (i + 1) * i // 2 + c + 1]
                gb[p, :, k] = gsi[c], gsi[i], bsi[c], bsi[i]
                sel[p, 0, k, c] = sel[p, 1, k, i] = 1
                mask[p, k] = p % PR < 4 * k + p // PR
    out |= {"wl": wl, "gb": gb, "sel": sel, "mask": mask}
    out["wlx"] = np.stack([wl_in[:, (i + 1) * i // 2] for i in range(PR)], axis=0)
    out["gbsi"] = np.stack([gsi, bsi], axis=1)
    glbl = np.stack([a["L0_rec_gl"][:KEPT], a["L0_rec_bl"][:KEPT]])
    out["glbl"] = np.ascontiguousarray(glbl.reshape(2, KEPT // P, P).transpose(2, 0, 1))
    w1 = np.concatenate([a["W_top1"][:KEPT], a["W_top1"][OUT:]], axis=0)
    out["w1"] = np.ascontiguousarray(w1.reshape(-1, P, H1).transpose(1, 0, 2))
    out["b1"] = np.ascontiguousarray(a["b_top1"].reshape(-1, P).T)
    out["w2"] = np.ascontiguousarray(a["W_top2"].reshape(-1, P, H2).transpose(1, 0, 2))
    out["b2"] = np.ascontiguousarray(a["b_top2"].reshape(-1, P).T)
    out["w3"] = np.ascontiguousarray(a["W_top3"].reshape(-1, P).T)
    return out


def kernel(**inputs):
    import concourse.bacc as bacc
    from concourse.bass_utils import run_bass_kernel_spmd

    nc = bacc.Bacc("TRN2", target_bir_lowering=False, num_devices=1)
    arrays = {f"{k}_dram": v for k, v in layouts(inputs).items()}
    t = {k[:-5]: nc.dram_tensor(k, v.shape, mybir.dt.from_np(v.dtype), kind="ExternalInput").ap()
         for k, v in arrays.items()}
    t["out"] = nc.dram_tensor("y_dram", (B, 1), F32, kind="ExternalOutput").ap()
    dlrm_tower(nc, t)
    r = run_bass_kernel_spmd(nc, [arrays], core_ids=[0])
    return r.results[0]["y_dram"]
```
